# Optimizing a Trainium2 kernel written in Bass

```python
import numpy as np
import jax
import jax.numpy as jnp

def _softmax(x, axis=-1):
    return jax.nn.softmax(x, axis=axis)

def _gelu(x):
    return jax.nn.gelu(x, approximate=True)

def _silu(x):
    return jax.nn.silu(x)

def _sigmoid(x):
    return jax.nn.sigmoid(x)

def _layernorm(x, axis=-1, eps=1e-05):
    m = jnp.mean(x, axis=axis, keepdims=True)
    v = jnp.var(x, axis=axis, keepdims=True)
    return (x - m) / jnp.sqrt(v + eps)

def _scatter_add(tgt, idx, src, axis=0):
    return tgt.at[idx].add(src)

def _segment_sum(src, seg, n):
    return jax.ops.segment_sum(src, seg, n)
kernel_name = 'mk_gnn_preln_d2_gnn_r64_4d40ad'

def setup_inputs(seed: int=0):
    np.random.seed(seed)
    _w = jnp.asarray

    def _rec_inputs():
        import jax
        import jax.numpy as jnp
        _gk = jax.random.key(seed)
        x = -0.000202 + 1 * jax.random.normal(jax.random.fold_in(_gk, 1), (100000, 64), jnp.float32)
        src = jax.random.randint(jax.random.fold_in(_gk, 2), (25000,), 0, 100000, jnp.int32)
        dst = jnp.minimum((100000 * jax.random.uniform(jax.random.fold_in(_gk, 3), (25000,)) ** 2.0).astype(jnp.int32), 99999)
        _o = jnp.argsort(dst, stable=True)
        src = src[_o]
        dst = dst[_o]
        edge_attr_8 = 0.00028786 + 0.999816 * jax.random.normal(jax.random.fold_in(_gk, 11), (25000, 8), jnp.float32)
        return (x, src, dst, edge_attr_8)
    x, src, dst, edge_attr_8 = _rec_inputs()

    def _L0_gnn_setup():
        import jax, jax.numpy as jnp
        import numpy as np
        N_NODES = 100000
        N_EDGES = 12500
        D = 64
        H = 4
        key = jax.random.key(seed)
        k1, k2, k3, k4, k5 = jax.random.split(key, 5)
        xavier = float(np.sqrt(2.0 / (D + D)))
        all_embeddings = jax.random.normal(k1, (N_NODES, D), dtype=jnp.float32)
        Wq = jax.random.normal(k2, (D, D), dtype=jnp.float32) * xavier
        Wk = jax.random.normal(k3, (D, D), dtype=jnp.float32) * xavier
        Wv = jax.random.normal(k4, (D, D), dtype=jnp.float32) * xavier
        edge_index = jax.random.randint(k5, (2, N_EDGES), 0, N_NODES, dtype=jnp.int32)
        return {'all_embeddings': all_embeddings, 'Wq': Wq, 'Wk': Wk, 'Wv': Wv, 'edge_index': edge_index}
    _L0_gnn_all = _L0_gnn_setup()
    _L0_gnn_in = {k: v for k, v in _L0_gnn_all.items() if k in ('Wq', 'Wk', 'Wv')}
    del _L0_gnn_all

    def _L1_gnn_setup():
        import jax, jax.numpy as jnp
        import numpy as np
        N_NODES = 100000
        N_EDGES = 18750
        D_IN = 64
        D_HID = 128
        D_OUT = 64

        def _glorot(key, fan_in, fan_out):
            lim = float(np.sqrt(6.0 / (fan_in + fan_out)))
            return jax.random.uniform(key, (fan_in, fan_out), jnp.float32, -lim, lim)

        def _sage_conv(x, src, dst, Wl, b, Wr, n_nodes):
            msg = x[src]
            ssum = jax.ops.segment_sum(msg, dst, num_segments=n_nodes)
            cnt = jax.ops.segment_sum(jnp.ones((src.shape[0],), x.dtype), dst, num_segments=n_nodes)[:, None]
            agg = jnp.where(cnt > 0, ssum / jnp.maximum(cnt, 1), 0.0)
            return agg @ Wl + b + x @ Wr
        key = jax.random.key(seed)
        ks = jax.random.split(key, 8)
        x = jax.random.normal(ks[0], (N_NODES, D_IN), jnp.float32)
        edge_index = jax.random.randint(ks[1], (2, N_EDGES), 0, N_NODES, jnp.int64)
        edge_attr = jax.random.normal(ks[2], (N_EDGES, 8), jnp.float32)
        W1l = _glorot(ks[3], D_IN, D_HID)
        b1 = jnp.zeros((D_HID,), jnp.float32)
        W1r = _glorot(ks[4], D_IN, D_HID)
        W2l = _glorot(ks[5], D_HID, D_OUT)
        b2 = jnp.zeros((D_OUT,), jnp.float32)
        W2r = _glorot(ks[6], D_HID, D_OUT)
        return {'x': x, 'edge_index': edge_index, 'edge_attr': edge_attr, 'W1l': W1l, 'b1': b1, 'W1r': W1r, 'W2l': W2l, 'b2': b2, 'W2r': W2r}
    _L1_gnn_all = _L1_gnn_setup()
    _L1_gnn_in = {k: v for k, v in _L1_gnn_all.items() if k in ('W1l', 'b1', 'W1r', 'W2l', 'b2', 'W2r')}
    del _L1_gnn_all
    return {'x': x, 'src': src, 'dst': dst, 'edge_attr_8': edge_attr_8, 'L0_gnn_Wq': _L0_gnn_in['Wq'], 'L0_gnn_Wk': _L0_gnn_in['Wk'], 'L0_gnn_Wv': _L0_gnn_in['Wv'], 'L1_gnn_W1l': _L1_gnn_in['W1l'], 'L1_gnn_b1': _L1_gnn_in['b1'], 'L1_gnn_W1r': _L1_gnn_in['W1r'], 'L1_gnn_W2l': _L1_gnn_in['W2l'], 'L1_gnn_b2': _L1_gnn_in['b2'], 'L1_gnn_W2r': _L1_gnn_in['W2r']}

def reference(x, src, dst, edge_attr_8, L0_gnn_Wq, L0_gnn_Wk, L0_gnn_Wv, L1_gnn_W1l, L1_gnn_b1, L1_gnn_W1r, L1_gnn_W2l, L1_gnn_b2, L1_gnn_W2r):
    import jax
    import jax.numpy as jnp

    def _L0_gnn_ref(all_embeddings, Wq, Wk, Wv, edge_index):
        import jax, jax.numpy as jnp
        import numpy as np
        N_NODES = 100000
        N_EDGES = 12500
        D = 64
        H = 4
        rows, cols = (edge_index[0], edge_index[1])
        n_nodes = all_embeddings.shape[0]
        e = rows.shape[0]
        dh = D // H
        row_emb = all_embeddings[rows]
        col_emb = all_embeddings[cols]
        q = (row_emb @ Wq).reshape(e, H, dh)
        k = (col_emb @ Wk).reshape(e, H, dh)
        v = (col_emb @ Wv).reshape(e, H, dh)
        att = jnp.einsum('ehd,ehd->eh', q, k)
        att = jnp.clip(att, -10.0, 10.0)
        exp_att = jnp.exp(att)
        att_norm = jax.ops.segment_sum(exp_att, rows, num_segments=n_nodes)
        att = exp_att / (att_norm[rows] + 1e-08)
        out_e = (att[:, :, None] * v).reshape(e, D)
        out = jax.ops.segment_sum(out_e, rows, num_segments=n_nodes)
        return out

    def _L1_gnn_ref(x, edge_index, edge_attr, W1l, b1, W1r, W2l, b2, W2r):
        import jax, jax.numpy as jnp
        import numpy as np
        N_NODES = 100000
        N_EDGES = 18750
        D_IN = 64
        D_HID = 128
        D_OUT = 64

        def _glorot(key, fan_in, fan_out):
            lim = float(np.sqrt(6.0 / (fan_in + fan_out)))
            return jax.random.uniform(key, (fan_in, fan_out), jnp.float32, -lim, lim)

        def _sage_conv(x, src, dst, Wl, b, Wr, n_nodes):
            msg = x[src]
            ssum = jax.ops.segment_sum(msg, dst, num_segments=n_nodes)
            cnt = jax.ops.segment_sum(jnp.ones((src.shape[0],), x.dtype), dst, num_segments=n_nodes)[:, None]
            agg = jnp.where(cnt > 0, ssum / jnp.maximum(cnt, 1), 0.0)
            return agg @ Wl + b + x @ Wr
        src, dst = (edge_index[0], edge_index[1])
        n = x.shape[0]
        h = jax.nn.relu(_sage_conv(x, src, dst, W1l, b1, W1r, n))
        out = _sage_conv(h, src, dst, W2l, b2, W2r, n)
        return out
    edge_index = jnp.stack([src, dst])
    h = jnp.maximum(_layernorm(x, axis=-1), 0.0)
    x = x + _L0_gnn_ref(h, L0_gnn_Wq, L0_gnn_Wk, L0_gnn_Wv, edge_index)
    h = jnp.maximum(_layernorm(x, axis=-1), 0.0)
    x = x + _L1_gnn_ref(h, edge_index, edge_attr_8, L1_gnn_W1l, L1_gnn_b1, L1_gnn_W1r, L1_gnn_W2l, L1_gnn_b2, L1_gnn_W2r)
    return x

_drawn_inputs = setup_inputs


def setup_inputs(seed=0):
    import zlib

    import numpy as np

    out = dict(_drawn_inputs(seed))
    spreads = {'L1_gnn_b1': (0.0, 0.1), 'L1_gnn_b2': (0.0, 0.1)}
    factors = {}
    for name, (base, spread) in spreads.items():
        noise = np.random.default_rng([zlib.crc32(name.encode()), seed]).standard_normal(out[name].shape)
        drawn = base * np.exp(spread * noise) if base else spread * noise
        out[name] = jnp.asarray(drawn.astype(out[name].dtype))
    for name, factor in factors.items():
        out[name] = (out[name] * factor).astype(out[name].dtype)
    return out
```

```python
import concourse.bass as bass
from concourse import mybir
from contextlib import ExitStack

N, E, D, HEADS, HID = 100000, 25000, 64, 4, 128
HD = D // HEADS
P = 128
COLS = -(-E // P)
TILES = 4
ROUNDS = COLS // TILES
W = D + HEADS
PAD_KEY = N + TILES * P
TABLE = -(-(PAD_KEY + 1) // (ROUNDS * P // 4)) * (ROUNDS * P // 4)
ROWS = 16
CHUNK = P * ROWS
FULL = N // CHUNK
TAIL = (N - FULL * CHUNK) // ROWS
NB = 4
PEEL = 5
EPS = 1e-5
assert COLS == ROUNDS * TILES and FULL + 1 == ROUNDS and FULL * CHUNK + TAIL * ROWS == N
assert (ROUNDS - PEEL) % NB == 0 and TABLE * W % (ROUNDS * P) == 0
ZW = TABLE * W // (ROUNDS * P)


class Chain:

    def __init__(self, eng, sem):
        self.eng, self.sem, self.n, self.g = eng, sem, 0, None

    def link(self, ins):
        ins.then_inc(self.sem, 1)
        self.n += 1
        self.eng.wait_ge(self.sem, self.n if self.g is None else self.g + self.n)


def rounds(eng, body, chain=None):
    start = chain.n if chain else 0
    for i in range(PEEL):
        body(i, i, 0)
    per = (chain.n - start) // PEEL if chain else 0
    with eng.Fori(0, (ROUNDS - PEEL) // NB) as g:
        for k in range(PEEL, PEEL + NB):
            if chain:
                chain.g, chain.n = g * (per * NB), start + per * k
            body(g * NB + k, k, g)
            if chain:
                assert chain.n == start + per * (k + 1)
    if chain:
        chain.g, chain.n = None, start + per * ROUNDS


def gnn_kernel(nc, x, src, dst, Wq, Wk, Wv, W1l, b1, W1r, W2l, b2, W2r, out):
    fp32, bf16, i32 = mybir.dt.float32, mybir.dt.bfloat16, mybir.dt.int32
    ALU, ACT, AX = mybir.AluOpType, mybir.ActivationFunctionType, mybir.AxisListType
    V, A, T = nc.vector, nc.scalar, nc.tensor

    ctx = ExitStack()
    with ctx:
        def sb(name, shape, dt=fp32):
            return ctx.enter_context(nc.sbuf_tensor(name, shape, dt))

        def pb(name, shape, dt=fp32):
            return ctx.enter_context(nc.psum_tensor(name, shape, dt))

        def sem(name):
            return ctx.enter_context(nc.semaphore(name))

        def two(make, name, *shape):
            return [make(f"{name}{n}", *shape) for n in range(2)]

        att_sums = nc.dram_tensor("att_sums", [TABLE, W], fp32).ap()
        agg_sums = nc.dram_tensor("agg_sums", [TABLE, W], fp32).ap()
        x1_dram = nc.dram_tensor("x1_dram", [N, D], fp32).ap()

        ident = sb("ident", [P, P])
        upper = sb("upper", [P, P])
        ones = sb("ones", [P, 1])
        zeros = sb("zeros", [P, ZW])
        eps = sb("eps", [P, 1])
        wqkv = sb("wqkv", [P, 3 * D])
        w1 = sb("w1", [P, HID])
        w2l = sb("w2l", [P, D])
        w2r = sb("w2r", [P, D])
        b1c = sb("b1c", [P, 1])
        b2f = sb("b2f", [3, D])
        b2part = sb("b2part", [3, 3, D], bf16)
        b2rest = sb("b2rest", [3, 2, D])
        b2sel = sb("b2sel", [3, D])
        b2rows = sb("b2rows", [3, 8, D], bf16)
        ones3 = sb("ones3", [3, P], bf16)

        src_key = sb("src_key", [P, ROUNDS, TILES], i32)
        dst_key = sb("dst_key", [P, ROUNDS, TILES], i32)
        spare = sb("spare", [P, ROUNDS, TILES], i32)
        both_keys = sb("both_keys", [P, ROUNDS + 1, 2 * TILES], i32)
        x_rows = sb("x_rows", [P, ROUNDS + 1, 2 * TILES], i32)
        src_f = sb("src_f", [P, ROUNDS, 2 * TILES])
        dst_f = sb("dst_f", [P, ROUNDS, 2 * TILES])
        dst_row = sb("dst_row", [P, ROUNDS, TILES], i32)
        edge = sb("edge", [P, COLS, D])

        key_col = two(sb, "key_col", [P, 2 * TILES])
        key_row = two(sb, "key_row", [P, TILES * P])
        same = two(sb, "same", [P, TILES, TILES * P])
        before = two(sb, "before", [P, TILES, P])
        pushed = sb("pushed", [P, TILES])
        sums = two(sb, "sums", [P, TILES, W])
        sums_out = two(sb, "sums_out", [P, TILES, D])
        sum_row = two(sb, "sum_row", [P, TILES], i32)

        stats = sb("stats", [P, ROWS, 6])
        mean2 = sb("mean2", [P, ROWS])
        diff = sb("diff", [P, ROWS])
        ssq = sb("ssq", [P, ROWS])
        ssq2 = sb("ssq2", [P, ROWS])
        logv = sb("logv", [P, ROWS])
        rstd = sb("rstd", [P, ROWS])

        rows_x = two(sb, "rows_x", [P, 2 * TILES], i32)
        rows_att = two(sb, "rows_att", [P, TILES], i32)
        rows_agg = two(sb, "rows_agg", [P, 2 * TILES], i32)
        x_pair = two(sb, "x_pair", [P, TILES, 2, D])
        att_got = two(sb, "att_got", [P, TILES, W])
        agg_got = two(sb, "agg_got", [P, 2 * TILES, W])

        h_mid = sb("h_mid", [P, TILES, 2, D])
        h_pair = sb("h_pair", [P, TILES, 2, D])
        hT = sb("hT", [P, TILES * P])
        q_sb = sb("q_sb", [P, TILES, D])
        qk = sb("qk", [P, TILES, D])
        att = sb("att", [P, TILES, HEADS])
        att_c = sb("att_c", [P, TILES, HEADS])
        vals = two(sb, "vals", [P, TILES, W])
        z_inv = sb("z_inv", [P, TILES, HEADS])
        x1_e = sb("x1_e", [P, TILES, D])
        h_e = two(sb, "h_e", [P, TILES, W])
        cat_e = two(sb, "cat_e", [P, TILES, 2, D])
        inv_e = two(sb, "inv_e", [P, 2 * TILES])

        xb = [sb(f"xb{n}", [P, ROWS, D]) for n in range(NB)]
        tb = [sb(f"tb{n}", [P, ROWS, W]) for n in range(NB)]
        zn = sb("zn", [P, ROWS, HEADS])
        mid = sb("mid", [P, ROWS, D])
        cat = two(sb, "cat", [P, ROWS, 2, D])
        inv_n = sb("inv_n", [P, ROWS])
        catT = two(sb, "catT", [P, 4 * P])
        gT = two(sb, "gT", [P, 4 * P])

        bank = pb("bank", [P, 8, 512])
        KEYS, HT, SUMS = bank[:, 0, :], bank[:, 1, :], [bank[:, 4, :], bank[:, 5, :]]
        QKV = bank[:, 2:4, 0:6 * D].rearrange("p a (t w) -> p a t w", t=2)
        COUNT = [bank[:, 6, 0:TILES], bank[:, 7, 0:TILES]]
        CATT, G, Y, MSG = bank[:, 2:4, :], [bank[:, 1, :], bank[:, 6, :]], bank[:, 4:6, :], bank[:, 7, :]

        s_w, s_keys = sem("weights_in"), sem("edges_in")
        s_fill, s_mask, s_ones = sem("filled"), sem("masks_made"), sem("constants_set")
        s_plain = sem("masks_filled")
        s_z0, s_z1, s_zo = sem("att_sums_zeroed"), sem("agg_sums_zeroed"), sem("spare_rows_zeroed")
        s_ready = sem("keys_ready")
        s_b2 = sem("b2_ready")
        v_step, a_step = sem("vector_step"), sem("scalar_step")
        key_staged, keys_T, key_rows = sem("key_staged"), sem("keys_transposed"), sem("key_rows_copied")
        same_done, count_done, sum_done = sem("same_done"), sem("count_done"), sem("sum_done")
        sums_ready, row_ready = sem("sums_ready"), sem("sum_row_ready")
        scattered = sem("scattered")
        waits_met = sem("waits_met")
        rx_ready, ra_ready, rg_ready = sem("rows_x_ready"), sem("rows_att_ready"), sem("rows_agg_ready")
        got_x, got_att, got_agg = two(sem, "got_x"), two(sem, "got_att"), two(sem, "got_agg")
        ssq_ready, rstd_ready = sem("ssq_ready"), sem("rstd_ready")
        h_ready, hT_done, hT_copied = sem("h_ready"), sem("hT_done"), sem("hT_copied")
        qkv_done, q_copied, att_ready, exp_ready = sem("qkv_done"), sem("q_copied"), sem("att_ready"), sem("exp_ready")
        vals_ready, kept_x, kept_h = sem("vals_ready"), sem("kept_x"), sem("kept_h")
        he_ready = sem("h_edge_ready")
        loaded = [sem(f"chunk_loaded{n}") for n in range(NB)]
        stored = [sem(f"chunk_stored{n}") for n in range(NB)]
        x1_ready = sem("x1_ready")
        cat_ready, cat_e_agg, cat_e_h = sem("cat_ready"), sem("cat_e_agg_ready"), sem("cat_e_h_ready")
        catT_done, catT_copied, g_done, g_ready = sem("catT_done"), sem("catT_copied"), sem("g_done"), sem("g_ready")
        w2_done = sem("w2_done")
        y_read, msg_ready = sem("y_read"), sem("messages_ready")

        def chunk_of(t, width):
            return t[0:FULL * CHUNK, :].rearrange("(c p r) w -> c p (r w)", p=P, r=ROWS), \
                t[FULL * CHUNK:N, :].rearrange("(p r) w -> p (r w)", r=ROWS)

        x_c, x_t = chunk_of(x, D)
        att_c_, att_t = chunk_of(att_sums, W)
        agg_c, agg_t = chunk_of(agg_sums, W)
        x1_c, x1_t = chunk_of(x1_dram, D)
        out_c, out_t = chunk_of(out, D)

        def bcast(col, inner):
            return col.unsqueeze(len(col.shape)).broadcast_to([*col.shape, inner])

        block = ctx.enter_context(nc.Block())

        @block.sync
        def _(sp):
            last = E - (P - 1) * COLS
            for key, given in ((src_key, src), (dst_key, dst)):
                flat = key[:].rearrange("p a b -> p (a b)")
                if key is src_key:
                    sp.wait_ge(s_fill, 2)
                sp.dma_start(flat[0:P - 1, :], given[0:(P - 1) * COLS].rearrange("(p c) -> p c", c=COLS)).then_inc(s_keys, 16)
                sp.dma_start(flat[P - 1:P, 0:last], given[(P - 1) * COLS:E].rearrange("(p c) -> p c", p=1)).then_inc(s_keys, 16)
            sp.wait_ge(s_fill, 3)
            for to, of in ((wqkv[0:D, 0:D], Wq), (wqkv[D:P, D:2 * D], Wk), (wqkv[D:P, 2 * D:3 * D], Wv),
                           (w1[0:D, :], W1l), (w1[D:P, :], W1r), (w2l[:, :], W2l), (w2r[:, :], W2r),
                           (b1c[:, :], b1.rearrange("(p a) -> p a", a=1)),
                           (b2f[:, :], b2.rearrange("(a n) -> a n", a=1).broadcast_to([3, D]))):
                sp.dma_start(to, of).then_inc(s_w, 16)
            sp.wait_ge(s_fill, 4)
            for table, s in ((att_sums, s_z0), (agg_sums, s_z1)):
                flat = table.rearrange("n w -> (n w)").rearrange("(c p f) -> c p f", c=ROUNDS, p=P)
                with sp.Fori(0, ROUNDS) as c:
                    sp.dma_start(flat[c], zeros[:, :]).then_inc(s, 16)
            sp.dma_start(out[N:TABLE, :].rearrange("(p r) w -> p (r w)", p=P), zeros[:, 0:(TABLE - N) * D // P]).then_inc(s_zo, 16)

            def load(k, c, whole, x_from, t_from):
                n = k % NB
                if whole:
                    sp.dma_start(xb[n][:].rearrange("p r w -> p (r w)"), x_from[0][c - 1]).then_inc(loaded[n], 16)
                    sp.dma_start(tb[n][:].rearrange("p r w -> p (r w)"), t_from[0][c - 1]).then_inc(loaded[n], 16)
                else:
                    sp.dma_start(xb[n][0:TAIL].rearrange("p r w -> p (r w)"), x_from[1]).then_inc(loaded[n], 16)
                    sp.dma_start(tb[n][0:TAIL].rearrange("p r w -> p (r w)"), t_from[1]).then_inc(loaded[n], 16)

            def stream(x_from, t_from, to, ready, per, before):
                load(0, 0, False, x_from, t_from)
                load(1, 1, True, x_from, t_from)

                def body(i, k, g):
                    if k + 2 >= NB:
                        sp.wait_ge(stored[(k + 2) % NB], (g + (k + 2 - NB) // NB + 1) * 16 + before[(k + 2) % NB])
                    load(k + 2, i + 2, True, x_from, t_from)
                    sp.wait_ge(ready, (i + 1) * per)
                    n = k % NB
                    sp.dma_start(to[0][i - 1] if k else to[1], xb[n][0:P if k else TAIL].rearrange("p r w -> p (r w)")).then_inc(stored[n], 16)

                for i in range(PEEL):
                    body(i, i, 0)
                with sp.Fori(0, (ROUNDS - PEEL) // NB - 1) as g:
                    for k in range(PEEL, PEEL + NB):
                        body(g * NB + k, k, g)
                for i in range(ROUNDS - NB, ROUNDS):
                    if i + 2 < ROUNDS:
                        body(i, i, 0)
                    else:
                        sp.wait_ge(ready, (i + 1) * per)
                        sp.dma_start(to[0][i - 1], xb[i % NB][:].rearrange("p r w -> p (r w)")).then_inc(stored[i % NB], 16)

            uses = [16 * len(range(n, ROUNDS, NB)) for n in range(NB)]
            sp.wait_ge(scattered, 64 * ROUNDS)
            stream((x_c, x_t), (att_c_, att_t), (x1_c, x1_t), x1_ready, 1, [0] * NB)
            for n in range(NB):
                sp.wait_ge(stored[n], uses[n])
            sp.wait_ge(scattered, 2 * 64 * ROUNDS)
            stream((x1_c, x1_t), (agg_c, agg_t), (out_c, out_t), y_read, 2, uses)
            for n in range(NB):
                sp.wait_ge(stored[n], 2 * uses[n])
            sp.wait_ge(s_zo, 16)

        @block.gpsimd
        def _(pool):
            G_ = nc.gpsimd
            G_.memset(src_key[:], PAD_KEY).then_inc(s_fill, 1)
            G_.memset(dst_key[:], PAD_KEY).then_inc(s_fill, 1)
            G_.memset(wqkv[:], 0.0).then_inc(s_fill, 1)
            G_.memset(zeros[:], 0.0).then_inc(s_fill, 1)
            G_.memset(ident[:], 0.0).then_inc(s_plain, 1)
            G_.memset(upper[:], 1.0).then_inc(s_plain, 1)
            G_.iota(spare[:], pattern=[[0, ROUNDS], [P, TILES]], base=N, channel_multiplier=1).then_inc(s_mask, 1)
            pool.wait_ge(s_plain, 2)
            G_.affine_select(out=ident[:], in_=ident[:], compare_op=ALU.not_equal, fill=1.0, base=0,
                             pattern=[[-1, P]], channel_multiplier=1).then_inc(s_mask, 1)
            G_.affine_select(out=upper[:], in_=upper[:], compare_op=ALU.is_gt, fill=0.0, base=0,
                             pattern=[[1, P]], channel_multiplier=-1).then_inc(s_mask, 1)

            def after_waits():
                pool.sem_inc(waits_met, 1)

            def gather(to, table, rows, c, s):
                pool.indirect_dma_start(out=to, out_offset=None, in_=table,
                                        in_offset=bass.IndirectOffsetOnAxis(ap=rows[:, c:c + 1], axis=0)).then_inc(s, 16)

            def scatter(b, k, table, of):
                pool.wait_ge(sums_ready, b + 1)
                pool.wait_ge(row_ready, b + 1)
                if k:
                    pool.wait_ge(scattered, 64 * b)
                after_waits()
                for j in range(TILES):
                    pool.indirect_dma_start(out=table, out_offset=bass.IndirectOffsetOnAxis(ap=sum_row[k % 2][:, j:j + 1], axis=0),
                                            in_=of[k % 2][:, j, :], in_offset=None, compute_op=ALU.add).then_inc(scattered, 16)

            def attention(i, k, g):
                pool.wait_ge(rx_ready, i + 1)
                if k >= 2:
                    pool.wait_ge(h_ready, i - 1)
                    pool.wait_ge(kept_x, i - 1)
                after_waits()
                for j in range(TILES):
                    for end in range(2):
                        gather(x_pair[k % 2][:, j, end, :], x, rows_x[k % 2], end * TILES + j, got_x[k % 2])
                if k == 1:
                    pool.wait_ge(s_z0, 16 * ROUNDS)
                if k:
                    scatter(i - 1, k - 1, att_sums, sums)

            rounds(pool, attention)
            scatter(ROUNDS - 1, ROUNDS - 1, att_sums, sums)

            pool.wait_ge(scattered, 64 * ROUNDS)
            pool.wait_ge(s_z1, 16 * ROUNDS)

            def sage(i, k, g):
                pool.wait_ge(ra_ready, i + 1)
                if k >= 2:
                    pool.wait_ge(he_ready, i - 1)
                after_waits()
                for j in range(TILES):
                    gather(att_got[k % 2][:, j, :], att_sums, rows_att[k % 2], j, got_att[k % 2])
                if k:
                    scatter(i - 1 + ROUNDS, k - 1 + ROUNDS, agg_sums, sums)

            rounds(pool, sage)
            scatter(2 * ROUNDS - 1, 2 * ROUNDS - 1, agg_sums, sums)

            pool.wait_ge(scattered, 2 * 64 * ROUNDS)

            def messages(i, k, g):
                pool.wait_ge(rg_ready, i + 1)
                if k >= 2:
                    pool.wait_ge(cat_e_agg, i - 1)
                after_waits()
                for j in range(2 * TILES):
                    gather(agg_got[k % 2][:, j, :], agg_sums, rows_agg[k % 2], j, got_agg[k % 2])

            rounds(pool, messages)

            for n in range(NB):
                pool.wait_ge(stored[n], 2 * 16 * len(range(n, ROUNDS, NB)))
            pool.wait_ge(s_zo, 16)
            rounds(pool, lambda i, k, g: scatter(i + 2 * ROUNDS, k + 2 * ROUNDS, out, sums_out))
            pool.wait_ge(scattered, 3 * 64 * ROUNDS)

        @block.vector
        def _(dve):
            chain = Chain(dve, v_step)
            link = chain.link

            V.memset(ones[:], 1.0).then_inc(s_ones, 1)
            V.memset(eps[:], EPS).then_inc(s_ones, 1)
            V.memset(ones3[:], 1.0).then_inc(s_ones, 1)
            V.memset(xb[0][:], 0.0).then_inc(s_ones, 1)
            V.memset(tb[0][:], 0.0).then_inc(s_ones, 1)
            for n in range(2):
                V.memset(h_e[n][:, :, D:W], 0.0).then_inc(s_ones, 1)
            dve.wait_ge(s_ones, 7)
            for n in range(2):
                V.memset(h_e[n][:, :, D:D + 1], 1.0).then_inc(s_ones, 1)
            dve.wait_ge(s_keys, 64)
            dve.wait_ge(s_mask, 3)
            V.memset(both_keys[:, ROUNDS, :], 0)
            V.memset(x_rows[:, ROUNDS, :], 0)
            for n, (key, f) in enumerate(((src_key, src_f), (dst_key, dst_f))):
                one = slice(n * TILES, (n + 1) * TILES)
                V.tensor_copy(f[:, :, 0:TILES], key[:])
                V.tensor_tensor(f[:, :, TILES:], spare[:], key[:], ALU.subtract)
                V.tensor_scalar(x_rows[:, 0:ROUNDS, one], key[:], float(N - 1), None, ALU.min)
                link(V.tensor_copy(both_keys[:, 0:ROUNDS, one], key[:]))

            dve.wait_ge(s_w, 16 * 9)
            link(V.tensor_copy(b2part[:, 0, :], b2f[:]))
            link(V.tensor_tensor(b2rest[:, 0, :], b2f[:], b2part[:, 0, :], ALU.subtract))
            link(V.tensor_copy(b2part[:, 1, :], b2rest[:, 0, :]))
            link(V.tensor_tensor(b2rest[:, 1, :], b2rest[:, 0, :], b2part[:, 1, :], ALU.subtract))
            link(V.tensor_copy(b2part[:, 2, :], b2rest[:, 1, :]))
            link(V.tensor_scalar(b2sel[:], b2part[:, 0, :], ident[0:3, 0:1], None, ALU.mult))
            for n in (1, 2):
                link(V.scalar_tensor_tensor(out=b2sel[:], in0=b2part[:, n, :], scalar=ident[0:3, n:n + 1], in1=b2sel[:],
                                            op0=ALU.mult, op1=ALU.add))
            V.tensor_copy(b2rows[:], b2sel[:].unsqueeze(1).broadcast_to([3, 8, D])).then_inc(s_b2, 1)

            def stage(rows, table, c, ready, width=2 * TILES):
                V.tensor_copy(rows[:], table[:, c, 0:width]).then_inc(ready, 1)

            stage(rows_x[0], x_rows, 0, rx_ready)

            def stage_keys(f, i, k):
                V.tensor_copy(key_col[k % 2][:], f[:, i, :]).then_inc(key_staged, 1)

            def compare(b, k, upto=False):
                dve.wait_ge(key_staged, b + 1)
                dve.wait_ge(key_rows, b + 1)
                if k >= 2:
                    dve.wait_ge(sum_done, b - 1)
                for j in range(TILES):
                    w = (j + 1) * P if upto else TILES * P
                    ins = V.tensor_scalar(same[k % 2][:, j, 0:w], key_row[k % 2][:, 0:w], key_col[k % 2][:, j:j + 1], None, ALU.is_equal)
                if upto:
                    ins.then_inc(same_done, 1)
                else:
                    link(ins)
                    diagonal = same[k % 2][:].rearrange("p j (i q) -> p (j i) q", i=TILES)[:, 0::TILES + 1, :]
                    V.tensor_tensor(before[k % 2][:], diagonal, upper[:].unsqueeze(1).broadcast_to([P, TILES, P]),
                                    ALU.mult).then_inc(same_done, 1)

            def target(b, k, keep=None):
                dve.wait_ge(count_done, b + 1)
                if k >= 2:
                    dve.wait_ge(scattered, 64 * (b - 1))
                count = COUNT[k % 2]
                key = key_col[k % 2]
                link(V.scalar_tensor_tensor(out=pushed[:], in0=count, scalar=1.0, in1=key[:, TILES:], op0=ALU.min, op1=ALU.mult))
                if keep is not None:
                    V.tensor_tensor(keep, pushed[:], key[:, 0:TILES], ALU.add)
                V.tensor_tensor(sum_row[k % 2][:], pushed[:], key[:, 0:TILES], ALU.add).then_inc(row_ready, 1)

            def statistics(of, n):
                for r in range(n):
                    ins = V.bn_stats(stats[:, r, :], of[:, r, :])
                link(ins)
                even, odd = stats[:, 0:n, 0:3], stats[:, 0:n, 3:6]
                V.tensor_tensor(mean2[:, 0:n], even[:, :, 1], odd[:, :, 1], ALU.add)
                V.tensor_tensor(ssq2[:, 0:n], even[:, :, 2], odd[:, :, 2], ALU.add)
                link(V.tensor_tensor(diff[:, 0:n], even[:, :, 1], odd[:, :, 1], ALU.subtract))
                link(V.scalar_tensor_tensor(out=diff[:, 0:n], in0=diff[:, 0:n], scalar=float(D // 4), in1=diff[:, 0:n], op0=ALU.mult, op1=ALU.mult))
                V.tensor_tensor(ssq[:, 0:n], ssq2[:, 0:n], diff[:, 0:n], ALU.add).then_inc(ssq_ready, 1)

            def normalise(of, to, middle, n, r):
                link(V.scalar_tensor_tensor(out=middle, in0=bcast(mean2[:, 0:n], D), scalar=-0.5, in1=of, op0=ALU.mult, op1=ALU.add))
                dve.wait_ge(rstd_ready, r + 1)
                return V.scalar_tensor_tensor(out=to, in0=middle, scalar=0.0, in1=bcast(rstd[:, 0:n], D), op0=ALU.max, op1=ALU.mult)

            def by_head(t):
                return t.rearrange("p t (h d) -> p t h d", h=HEADS)

            def attention(i, k, g):
                u = k % 2
                stage(rows_x[(k + 1) % 2], x_rows, i + 1, rx_ready)
                stage_keys(src_f, i, k)
                dve.wait_ge(got_x[u], (g * (NB // 2) + k // 2 + 1) * 128)
                pair = x_pair[u][:].rearrange("p j e d -> p (j e) d")
                statistics(pair, 2 * TILES)
                compare(i, k)
                normalise(pair, h_pair[:].rearrange("p j e d -> p (j e) d"), h_mid[:].rearrange("p j e d -> p (j e) d"),
                          2 * TILES, i).then_inc(h_ready, 1)
                target(i, k)
                dve.wait_ge(qkv_done, i + 1)
                dve.wait_ge(q_copied, i + 1)
                link(V.tensor_tensor(qk[:].rearrange("p (a t) d -> p a t d", a=2), QKV[:, :, :, D:2 * D],
                                     q_sb[:].rearrange("p (a t) d -> p a t d", a=2), ALU.mult))
                link(V.reduce_sum(att[:], by_head(qk[:]), axis=AX.X))
                V.tensor_scalar(att_c[:], att[:], 10.0, -10.0, ALU.min, ALU.max).then_inc(att_ready, 1)
                dve.wait_ge(exp_ready, i + 1)
                for a in range(2):
                    two_tiles = slice(2 * a, 2 * a + 2)
                    ins = V.tensor_tensor(by_head(vals[u][:, two_tiles, 0:D]), by_head(QKV[:, a, :, 2 * D:3 * D]),
                                          bcast(vals[u][:, two_tiles, D:W], HD), ALU.mult)
                ins.then_inc(vals_ready, 1)

            rounds(dve, attention, chain)

            stage(rows_att[0], both_keys, 0, ra_ready, TILES)
            dve.wait_ge(kept_x, ROUNDS)

            def sage(i, k, g):
                u, n, b, kb = k % 2, k % NB, i + ROUNDS, k + ROUNDS
                stage(rows_att[(k + 1) % 2], both_keys, i + 1, ra_ready, TILES)
                stage_keys(dst_f, i, kb)
                dve.wait_ge(loaded[n], (g + k // NB + 1) * 32)
                link(V.tensor_scalar(zn[:], tb[n][:, :, D:W], 1e-8, None, ALU.add))
                link(V.reciprocal(zn[:], zn[:]))
                link(V.tensor_tensor(by_head(tb[n][:, :, 0:D]), by_head(tb[n][:, :, 0:D]), bcast(zn[:], HD), ALU.mult))
                V.tensor_tensor(xb[n][:], xb[n][:], tb[n][:, :, 0:D], ALU.add).then_inc(x1_ready, 1)
                dve.wait_ge(got_att[u], (g * (NB // 2) + k // 2 + 1) * 64)
                link(V.tensor_scalar(z_inv[:], att_got[u][:, :, D:W], 1e-8, None, ALU.add))
                link(V.reciprocal(z_inv[:], z_inv[:]))
                link(V.tensor_tensor(by_head(x1_e[:]), by_head(att_got[u][:, :, 0:D]), bcast(z_inv[:], HD), ALU.mult))
                link(V.tensor_tensor(x1_e[:], x1_e[:], edge[:, bass.ts(i, TILES), :], ALU.add))
                statistics(x1_e[:], TILES)
                compare(b, kb)
                if k >= 2:
                    dve.wait_ge(kept_h, i - 1)
                normalise(x1_e[:], h_e[u][:, :, 0:D], h_mid[:, :, 0, :], TILES, b).then_inc(he_ready, 1)
                target(b, kb, dst_row[:, i, :])

            rounds(dve, sage, chain)

            stage(rows_agg[0], both_keys, 0, rg_ready)

            def products_to_output(i, k):
                n = k % NB
                for half in range(2):
                    rows8 = slice(8 * half, 8 * half + 8)
                    dve.wait_ge(w2_done, i * 5 + 2 * half + 2)
                    V.tensor_tensor(xb[n][:, rows8, :], xb[n][:, rows8, :], Y[:, half, :].rearrange("p (r d) -> p r d", d=D),
                                    ALU.add).then_inc(y_read, 1)
                dve.wait_ge(w2_done, i * 5 + 5)
                V.tensor_tensor(edge[:, bass.ts(i, TILES), :], MSG[:, 0:TILES * D].rearrange("p (t d) -> p t d", d=D),
                                bcast(inv_e[k % 2][:, TILES:], D), ALU.mult).then_inc(msg_ready, 1)

            def messages(i, k, g):
                u, n = k % 2, k % NB
                stage(rows_agg[(k + 1) % 2], both_keys, i + 1, rg_ready)
                dve.wait_ge(loaded[n], (g + k // NB + 1) * 32 + 32 * len(range(n, ROUNDS, NB)))
                statistics(xb[n][:], ROWS)
                link(V.tensor_scalar(inv_n[:], tb[n][:, :, D], 1.0, None, ALU.max))
                link(V.reciprocal(inv_n[:], inv_n[:]))
                if k >= 2:
                    dve.wait_ge(catT_done, i * 5 - 6)
                V.tensor_tensor(cat[u][:, :, 0, :], tb[n][:, :, 0:D], bcast(inv_n[:], D), ALU.mult)
                normalise(xb[n][:], cat[u][:, :, 1, :], mid[:], ROWS, i + 2 * ROUNDS).then_inc(cat_ready, 1)
                dve.wait_ge(got_agg[u], (g * (NB // 2) + k // 2 + 1) * 128)
                link(V.tensor_scalar(inv_e[u][:], agg_got[u][:, :, D], 1.0, None, ALU.max))
                link(V.reciprocal(inv_e[u][:], inv_e[u][:]))
                if k >= 2:
                    dve.wait_ge(catT_done, i * 5 - 5)
                V.tensor_tensor(cat_e[u][:, :, 0, :], agg_got[u][:, 0:TILES, 0:D], bcast(inv_e[u][:, 0:TILES], D),
                                ALU.mult).then_inc(cat_e_agg, 1)
                if k:
                    products_to_output(i - 1, k - 1)

            rounds(dve, messages, chain)
            products_to_output(ROUNDS - 1, ROUNDS - 1)

            def last_sums(i, k, g):
                b, kb = i + 2 * ROUNDS, k + 2 * ROUNDS
                stage_keys(dst_f, i, kb)
                dve.wait_ge(scattered, 64 * (b - 1))
                V.tensor_copy(sum_row[kb % 2][:], dst_row[:, i, :]).then_inc(row_ready, 1)
                compare(b, kb, upto=True)

            rounds(dve, last_sums, chain)

        @block.scalar
        def _(act):
            chain = Chain(act, a_step)

            def copy_keys(b, k):
                act.wait_ge(keys_T, b + 1)
                if k >= 2:
                    act.wait_ge(same_done, b - 1)
                A.copy(key_row[k % 2][:], KEYS[:, :]).then_inc(key_rows, 1)

            def rsqrt(n, r):
                act.wait_ge(ssq_ready, r + 1)
                chain.link(A.activation(logv[:, 0:n], ssq[:, 0:n], ACT.Ln, bias=eps[:, 0:1], scale=1.0 / D))
                A.activation(rstd[:, 0:n], logv[:, 0:n], ACT.Exp, scale=-0.5).then_inc(rstd_ready, 1)

            def copy_sums(b, k, to, width):
                act.wait_ge(sum_done, b + 1)
                if k >= 2:
                    act.wait_ge(scattered, 64 * (b - 1))
                A.copy(to[k % 2][:].rearrange("p t w -> p (t w)"), SUMS[k % 2][:, 0:TILES * width]).then_inc(sums_ready, 1)

            A.preload_act_table_set("natural_log_exp_and_others")
            act.wait_ge(s_ones, 9)

            def attention(i, k, g):
                u = k % 2
                act.wait_ge(got_x[u], (g * (NB // 2) + k // 2 + 1) * 128)
                A.copy(edge[:, bass.ts(i, TILES), :], x_pair[u][:, :, 0, :]).then_inc(kept_x, 1)
                copy_keys(i, k)
                rsqrt(2 * TILES, i)
                act.wait_ge(hT_done, i + 1)
                if k:
                    act.wait_ge(qkv_done, i)
                A.copy(hT[:], HT[:, :]).then_inc(hT_copied, 1)
                act.wait_ge(qkv_done, i + 1)
                if k:
                    act.wait_ge(att_ready, i)
                A.copy(q_sb[:].rearrange("p (a t) d -> p a t d", a=2), QKV[:, :, :, 0:D]).then_inc(q_copied, 1)
                act.wait_ge(att_ready, i + 1)
                if k >= 2:
                    act.wait_ge(sum_done, i - 1)
                A.activation(vals[u][:, :, D:W], att_c[:], ACT.Exp).then_inc(exp_ready, 1)
                copy_sums(i, k, sums, W)

            rounds(act, attention, chain)

            def sage(i, k, g):
                copy_keys(i + ROUNDS, k + ROUNDS)
                rsqrt(TILES, i + ROUNDS)
                act.wait_ge(he_ready, i + 1)
                A.copy(edge[:, bass.ts(i, TILES), :], h_e[k % 2][:, :, 0:D]).then_inc(kept_h, 1)
                copy_sums(i + ROUNDS, k + ROUNDS, sums, W)

            rounds(act, sage, chain)
            act.wait_ge(kept_h, ROUNDS)

            def group(i, k, q):
                n, kn = i * 5 + q, k * 5 + q
                act.wait_ge(catT_done, n + 1)
                if kn >= 2:
                    act.wait_ge(g_done, n - 1)
                A.copy(catT[kn % 2][:], CATT[:, kn % 2, :]).then_inc(catT_copied, 1)
                if kn:
                    relu(n - 1, kn - 1)

            def relu(n, kn):
                act.wait_ge(g_done, n + 1)
                if kn >= 2:
                    act.wait_ge(w2_done, n - 1)
                A.activation(gT[kn % 2][:], G[kn % 2], ACT.Relu, bias=b1c[:, 0:1]).then_inc(g_ready, 1)

            act.wait_ge(s_w, 16 * 9)

            def messages(i, k, g):
                if k:
                    group(i - 1, k - 1, 0)
                rsqrt(ROWS, i + 2 * ROUNDS)
                if k >= 2:
                    act.wait_ge(catT_done, i * 5 - 5)
                A.copy(cat_e[k % 2][:, :, 1, :], edge[:, bass.ts(i, TILES), :]).then_inc(cat_e_h, 1)
                for q in range(1, 5):
                    if k:
                        group(i - 1, k - 1, q)

            rounds(act, messages, chain)
            for q in range(5):
                group(ROUNDS - 1, ROUNDS - 1, q)
            relu(5 * ROUNDS - 1, 5 * ROUNDS - 1)

            def last_sums(i, k, g):
                copy_keys(i + 2 * ROUNDS, k + 2 * ROUNDS)
                copy_sums(i + 2 * ROUNDS, k + 2 * ROUNDS, sums_out, D)

            rounds(act, last_sums, chain)

        @block.tensor
        def _(pe):
            def transpose_keys(b, k):
                pe.wait_ge(key_staged, b + 1)
                if k:
                    pe.wait_ge(key_rows, b)
                for j in range(TILES):
                    ins = T.transpose(KEYS[:, j * P:(j + 1) * P], key_col[k % 2][:, j:j + 1].broadcast_to([P, P]), ident[:])
                ins.then_inc(keys_T, 1)

            def counts(b, k):
                pe.wait_ge(same_done, b + 1)
                if k >= 2:
                    pe.wait_ge(row_ready, b - 1)
                for i in range(TILES):
                    to = COUNT[k % 2][:, i:i + 1]
                    for j in range(i):
                        T.matmul(to, same[k % 2][:, j, i * P:(i + 1) * P], ones[:], start=(j == 0), stop=False)
                    ins = T.matmul(to, before[k % 2][:, i, :], ones[:], start=(i == 0), stop=True)
                ins.then_inc(count_done, 1)

            def sum_up(b, k, values, width):
                if k >= 2:
                    pe.wait_ge(sums_ready, b - 1)
                for i in range(TILES):
                    for j in range(i, TILES):
                        ins = T.matmul(SUMS[k % 2][:, i * width:(i + 1) * width], same[k % 2][:, j, i * P:(i + 1) * P],
                                       values(j), start=(j == i), stop=(j == TILES - 1))
                ins.then_inc(sum_done, 1)

            pe.wait_ge(s_mask, 3)
            pe.wait_ge(s_ones, 9)
            pe.wait_ge(s_w, 16 * 9)

            def attention(i, k, g):
                u = k % 2
                transpose_keys(i, k)
                counts(i, k)
                pe.wait_ge(h_ready, i + 1)
                if k:
                    pe.wait_ge(hT_copied, i)
                for j in range(TILES):
                    ins = T.transpose(HT[:, j * P:(j + 1) * P], h_pair[:, j].rearrange("p e d -> p (e d)"), ident[:])
                ins.then_inc(hT_done, 1)
                pe.wait_ge(hT_copied, i + 1)
                if k:
                    pe.wait_ge(vals_ready, i)
                for j in range(TILES):
                    ins = T.matmul(QKV[:, j // 2, j % 2, :], hT[:, j * P:(j + 1) * P], wqkv[:], start=True, stop=True)
                ins.then_inc(qkv_done, 1)
                pe.wait_ge(vals_ready, i + 1)
                sum_up(i, k, lambda j: vals[u][:, j, :], W)

            rounds(pe, attention)

            def sage(i, k, g):
                transpose_keys(i + ROUNDS, k + ROUNDS)
                counts(i + ROUNDS, k + ROUNDS)
                pe.wait_ge(he_ready, i + 1)
                sum_up(i + ROUNDS, k + ROUNDS, lambda j: h_e[k % 2][:, j, :], W)

            rounds(pe, sage)

            pe.wait_ge(sums_ready, 2 * ROUNDS)
            pe.wait_ge(row_ready, 2 * ROUNDS)
            pe.wait_ge(s_b2, 1)

            def times_w1(n, kn):
                pe.wait_ge(catT_copied, n + 1)
                if kn >= 2:
                    pe.wait_ge(g_ready, n - 1)
                T.matmul(G[kn % 2], w1[:], catT[kn % 2][:], start=True, stop=True).then_inc(g_done, 1)

            def times_w2(i, k, q):
                n, kn = i * 5 + q, k * 5 + q
                pe.wait_ge(g_ready, n + 1)
                if q == 4:
                    if k:
                        pe.wait_ge(msg_ready, i)
                    for t in range(4):
                        ins = T.matmul(MSG[:, t * D:(t + 1) * D], gT[kn % 2][:, t * P:(t + 1) * P], w2l[:], start=True, stop=True)
                else:
                    half = q // 2
                    if q % 2 == 0:
                        if k:
                            pe.wait_ge(y_read, i * 2 + half - 1)
                        T.matmul(Y[:, half, :], ones3[:], b2rows[:].rearrange("p a d -> p (a d)"), start=True, stop=False)
                    for t in range(4):
                        at = (q % 2 * 4 + t) * D
                        ins = T.matmul(Y[:, half, at:at + D], gT[kn % 2][:, t * P:(t + 1) * P], w2r[:], start=False,
                                       stop=(q % 2 == 1 and t == 3))
                ins.then_inc(w2_done, 1)

            def messages(i, k, g):
                for q in range(5):
                    n, kn = i * 5 + q, k * 5 + q
                    if q < 4:
                        of = [cat[k % 2][:, 4 * q + t] for t in range(4)]
                        if q == 0:
                            pe.wait_ge(cat_ready, i + 1)
                    else:
                        of = [cat_e[k % 2][:, t] for t in range(4)]
                        pe.wait_ge(cat_e_agg, i + 1)
                        pe.wait_ge(cat_e_h, i + 1)
                    if kn >= 2:
                        pe.wait_ge(catT_copied, n - 1)
                    for t in range(4):
                        ins = T.transpose(CATT[:, kn % 2, t * P:(t + 1) * P], of[t].rearrange("p e d -> p (e d)"), ident[:])
                    ins.then_inc(catT_done, 1)
                    if kn >= 1:
                        times_w1(n - 1, kn - 1)
                    if kn >= 2:
                        if q >= 2:
                            times_w2(i, k, q - 2)
                        else:
                            times_w2(i - 1, k - 1, q + 3)

            rounds(pe, messages)
            times_w1(5 * ROUNDS - 1, 5 * ROUNDS - 1)
            times_w2(ROUNDS - 1, ROUNDS - 1, 3)
            times_w2(ROUNDS - 1, ROUNDS - 1, 4)

            pe.wait_ge(y_read, 2 * ROUNDS)
            pe.wait_ge(msg_ready, ROUNDS)

            def last_sums(i, k, g):
                b, kb = i + 2 * ROUNDS, k + 2 * ROUNDS
                transpose_keys(b, kb)
                pe.wait_ge(same_done, b + 1)
                sum_up(b, kb, lambda j: edge[:, i * TILES + j, :], D)

            rounds(pe, last_sums)


_INS = ["x", "src", "dst", "L0_gnn_Wq", "L0_gnn_Wk", "L0_gnn_Wv", "L1_gnn_W1l", "L1_gnn_b1", "L1_gnn_W1r",
        "L1_gnn_W2l", "L1_gnn_b2", "L1_gnn_W2r"]


def kernel(**inputs):
    import numpy as np
    import concourse.bacc as bacc
    from concourse.bass_utils import run_bass_kernel_spmd

    nc = bacc.Bacc("TRN2", target_bir_lowering=False, num_devices=1)
    arrays, args = {}, []
    for name in _INS:
        a = np.ascontiguousarray(inputs[name])
        arrays[f"in_{name}"] = a
        args.append(nc.dram_tensor(f"in_{name}", a.shape, mybir.dt.from_np(a.dtype), kind="ExternalInput").ap())
    out = nc.dram_tensor("out", (TABLE, D), mybir.dt.float32, kind="ExternalOutput").ap()
    gnn_kernel(nc, *args, out)
    r = run_bass_kernel_spmd(nc, [arrays], core_ids=[0])
    return r.results[0]["out"][0:N]
```

```python
import concourse.bass as bass
from concourse import mybir
from contextlib import ExitStack

N, E, D, HEADS, HID = 100000, 25000, 64, 4, 128
HD = D // HEADS
P = 128
COLS = -(-E // P)
TILES = 4
ROUNDS = COLS // TILES
W = D + HEADS
PAD_KEY = N + TILES * P
TABLE = -(-(PAD_KEY + 1) // (ROUNDS * P // 4)) * (ROUNDS * P // 4)
ROWS = 16
CHUNK = P * ROWS
FULL = N // CHUNK
TAIL = (N - FULL * CHUNK) // ROWS
NB = 4
LEAD = 3
PEEL = 5
EPS = 1e-5
assert COLS == ROUNDS * TILES and FULL + 1 == ROUNDS and FULL * CHUNK + TAIL * ROWS == N
assert (ROUNDS - PEEL) % NB == 0 and TABLE * W % (ROUNDS * P) == 0
ZW = TABLE * W // (ROUNDS * P)


class Chain:

    def __init__(self, eng, sem):
        self.eng, self.sem, self.n, self.g = eng, sem, 0, None

    def link(self, ins):
        self.wait(self.mark(ins))

    def mark(self, ins):
        ins.then_inc(self.sem, 1)
        self.n += 1
        return self.n

    def wait(self, n):
        self.eng.wait_ge(self.sem, n if self.g is None else self.g + n)


def rounds(eng, body, chain=None, first=0):
    start = chain.n - first if chain else 0
    for i in range(PEEL):
        body(i, i, 0)
    per = (chain.n - start) // PEEL if chain else 0
    with eng.Fori(0, (ROUNDS - PEEL) // NB) as g:
        for k in range(PEEL, PEEL + NB):
            if chain:
                chain.g, chain.n = g * (per * NB), start + per * k
            body(g * NB + k, k, g)
            if chain:
                assert chain.n == start + per * (k + 1)
    if chain:
        chain.g, chain.n = None, start + per * ROUNDS


def gnn_kernel(nc, x, src, dst, Wq, Wk, Wv, W1l, b1, W1r, W2l, b2, W2r, out):
    fp32, bf16, i32 = mybir.dt.float32, mybir.dt.bfloat16, mybir.dt.int32
    ALU, ACT, AX = mybir.AluOpType, mybir.ActivationFunctionType, mybir.AxisListType
    V, A, T = nc.vector, nc.scalar, nc.tensor

    ctx = ExitStack()
    with ctx:
        def sb(name, shape, dt=fp32):
            return ctx.enter_context(nc.sbuf_tensor(name, shape, dt))

        def pb(name, shape, dt=fp32):
            return ctx.enter_context(nc.psum_tensor(name, shape, dt))

        def sem(name):
            return ctx.enter_context(nc.semaphore(name))

        def two(make, name, *shape):
            return [make(f"{name}{n}", *shape) for n in range(2)]

        def ring(make, name, *shape):
            return [make(f"{name}{n}", *shape) for n in range(NB)]

        att_sums = nc.dram_tensor("att_sums", [TABLE, W], fp32).ap()
        agg_sums = nc.dram_tensor("agg_sums", [TABLE, W], fp32).ap()
        x1_dram = nc.dram_tensor("x1_dram", [N, D], fp32).ap()

        ident = sb("ident", [P, P])
        upto = sb("upto", [P, TILES * P])
        work = sb("work", [P, ZW])
        zeros = work[:, :]
        mid = work[:, 0:ROWS * D].rearrange("p (r d) -> p r d", d=D)
        eps = sb("eps", [P, 1])
        wqkv = sb("wqkv", [P, 3 * D])
        w1 = sb("w1", [P, HID])
        w2l = sb("w2l", [P, D])
        w2r = sb("w2r", [P, D])
        b1c = sb("b1c", [P, 1])
        b2f = sb("b2f", [3, D])
        b2part = sb("b2part", [3, 3, D], bf16)
        b2rest = sb("b2rest", [3, 2, D])
        b2sel = sb("b2sel", [3, D])
        b2rows = sb("b2rows", [3, 8, D], bf16)
        ones3 = sb("ones3", [3, P], bf16)

        src_key = sb("src_key", [P, ROUNDS, TILES], i32)
        dst_key = sb("dst_key", [P, ROUNDS, TILES], i32)
        spare = sb("spare", [P, ROUNDS, TILES], i32)
        both_keys = sb("both_keys", [P, ROUNDS + LEAD, 2 * TILES], i32)
        x_rows = sb("x_rows", [P, ROUNDS + LEAD, 2 * TILES], i32)
        keys_f = sb("keys_f", [P, 2 * ROUNDS + 1, 2 * TILES])
        dst_row = sb("dst_row", [P, ROUNDS, TILES], i32)
        edge = sb("edge", [P, COLS, D])
        agg = sb("agg", [P, COLS, D])
        inv_dst = sb("inv_dst", [P, ROUNDS, TILES])

        key_col = two(sb, "key_col", [P, 2 * TILES])
        key_row = two(sb, "key_row", [P, TILES * P])
        same = two(sb, "same", [P, TILES, TILES * P])
        count = sb("count", [P, TILES])
        pushed = sb("pushed", [P, TILES])
        sums = ring(sb, "sums", [P, TILES, W])
        sums_out = [s[:].rearrange("p t w -> p (t w)")[:, 0:TILES * D].rearrange("p (t d) -> p t d", d=D) for s in sums]
        sum_row = ring(sb, "sum_row", [P, TILES], i32)

        stats = sb("stats", [P, ROWS, 6])
        mean2 = sb("mean2", [P, ROWS])
        diff = sb("diff", [P, ROWS])
        ssq = sb("ssq", [P, ROWS])
        ssq2 = sb("ssq2", [P, ROWS])
        logv = sb("logv", [P, ROWS])
        rstd = sb("rstd", [P, ROWS])

        rows_x = ring(sb, "rows_x", [P, 2 * TILES], i32)
        rows_att = ring(sb, "rows_att", [P, TILES], i32)
        rows_agg = ring(sb, "rows_agg", [P, 2 * TILES], i32)
        agg_got = ring(sb, "agg_got", [P, 2 * TILES, W])
        x_pair = [t[:].rearrange("p j w -> p (j w)")[:, 0:TILES * 2 * D].rearrange("p (j e d) -> p j e d", e=2, d=D) for t in agg_got]
        att_got = [t[:, 0:TILES, :] for t in agg_got]

        catT = two(sb, "catT", [P, 4 * P])
        gT = two(sb, "gT", [P, 4 * P])
        h_mid, h_pair = (t[:].rearrange("p (j e d) -> p j e d", e=2, d=D) for t in gT)
        hT = catT[0]
        q_sb = sb("q_sb", [P, TILES, D])
        qk = sb("qk", [P, TILES, D])
        att = sb("att", [P, TILES, HEADS])
        att_c = sb("att_c", [P, TILES, HEADS])
        vals = two(sb, "vals", [P, TILES, W])
        z_inv = sb("z_inv", [P, TILES, HEADS])
        x1_e = sb("x1_e", [P, TILES, D])
        h_e = two(sb, "h_e", [P, TILES, W])
        inv_e = sb("inv_e", [P, 2 * TILES])
        msg = [t[:].rearrange("p t w -> p (t w)")[:, 0:TILES * D].rearrange("p (t d) -> p t d", d=D) for t in vals]

        xb = [sb(f"xb{n}", [P, ROWS, D]) for n in range(NB)]
        tb = [sb(f"tb{n}", [P, ROWS, W]) for n in range(NB)]
        cat_e = [t[:].rearrange("p r w -> p (r w)")[:, 0:TILES * 2 * D].rearrange("p (j e d) -> p j e d", e=2, d=D) for t in tb[0:2]]
        zn = sb("zn", [P, ROWS, HEADS])
        cat = [same[n][:].rearrange("p j (r e d) -> p (j r) e d", e=2, d=D) for n in range(2)]
        inv_n = sb("inv_n", [P, ROWS])

        bank = pb("bank", [P, 8, 512])
        KEYS, HT, SUMS = bank[:, 0, :], bank[:, 1, :], [bank[:, 4, :], bank[:, 5, :]]
        QKV = bank[:, 2:4, 0:6 * D].rearrange("p a (t w) -> p a t w", t=2)
        CATT, G, Y = bank[:, 2:4, :], [bank[:, 1, :], bank[:, 6, :]], [bank[:, 7, :], bank[:, 5, :]]
        MSG = [bank[:, 6, :], bank[:, 7, :]]

        s_w, s_keys = sem("weights_in"), sem("edges_in")
        s_fill, s_mask, s_ones = sem("filled"), sem("masks_made"), sem("constants_set")
        s_plain = sem("masks_filled")
        s_z0, s_z1, s_zo = sem("att_sums_zeroed"), sem("agg_sums_zeroed"), sem("spare_rows_zeroed")
        s_ready = sem("keys_ready")
        s_b2 = sem("b2_ready")
        v_step, a_step = sem("vector_step"), sem("scalar_step")
        key_staged, keys_T, key_rows = sem("key_staged"), sem("keys_transposed"), sem("key_rows_copied")
        same_done, sum_done = sem("same_done"), sem("sum_done")
        sums_ready, row_ready = sem("sums_ready"), sem("sum_row_ready")
        scattered = sem("scattered")
        waits_met = sem("waits_met")
        rx_ready, ra_ready, rg_ready = sem("rows_x_ready"), sem("rows_att_ready"), sem("rows_agg_ready")
        got_x, got_att, got_agg = ring(sem, "got_x"), ring(sem, "got_att"), ring(sem, "got_agg")
        ssq_ready, rstd_ready = sem("ssq_ready"), sem("rstd_ready")
        h_ready, hT_done, hT_copied = sem("h_ready"), sem("hT_done"), sem("hT_copied")
        qkv_done, q_copied, att_ready, exp_ready = sem("qkv_done"), sem("q_copied"), sem("att_ready"), sem("exp_ready")
        vals_ready, kept_x, kept_h = sem("vals_ready"), sem("kept_x"), sem("kept_h")
        he_ready = sem("h_edge_ready")
        loaded = [sem(f"chunk_loaded{n}") for n in range(NB)]
        stored = [sem(f"chunk_stored{n}") for n in range(NB)]
        x1_ready = sem("x1_ready")
        cat_ready, cat_e_agg, cat_e_h = sem("cat_ready"), sem("cat_e_agg_ready"), sem("cat_e_h_ready")
        catT_done, catT_copied, g_done, g_ready = sem("catT_done"), sem("catT_copied"), sem("g_done"), sem("g_ready")
        w2_done = sem("w2_done")
        y_read, msg_ready, agg_kept = sem("y_read"), sem("messages_ready"), sem("agg_kept")
        msgT_done, msgT_copied = sem("edge_catT_done"), sem("edge_catT_copied")
        eg_done, eg_ready, w2l_done = sem("edge_g_done"), sem("edge_g_ready"), sem("w2l_done")

        def chunk_of(t, width):
            return t[0:FULL * CHUNK, :].rearrange("(c p r) w -> c p (r w)", p=P, r=ROWS), \
                t[FULL * CHUNK:N, :].rearrange("(p r) w -> p (r w)", r=ROWS)

        x_c, x_t = chunk_of(x, D)
        att_c_, att_t = chunk_of(att_sums, W)
        agg_c, agg_t = chunk_of(agg_sums, W)
        x1_c, x1_t = chunk_of(x1_dram, D)
        out_c, out_t = chunk_of(out, D)

        def bcast(col, inner):
            return col.unsqueeze(len(col.shape)).broadcast_to([*col.shape, inner])

        block = ctx.enter_context(nc.Block())

        @block.sync
        def _(sp):
            last = E - (P - 1) * COLS
            for key, given in ((src_key, src), (dst_key, dst)):
                flat = key[:].rearrange("p a b -> p (a b)")
                if key is src_key:
                    sp.wait_ge(s_fill, 2)
                sp.dma_start(flat[0:P - 1, :], given[0:(P - 1) * COLS].rearrange("(p c) -> p c", c=COLS)).then_inc(s_keys, 16)
                sp.dma_start(flat[P - 1:P, 0:last], given[(P - 1) * COLS:E].rearrange("(p c) -> p c", p=1)).then_inc(s_keys, 16)
            sp.wait_ge(s_fill, 3)
            for to, of in ((wqkv[0:D, 0:D], Wq), (wqkv[D:P, D:2 * D], Wk), (wqkv[D:P, 2 * D:3 * D], Wv),
                           (w1[0:D, :], W1l), (w1[D:P, :], W1r), (w2l[:, :], W2l), (w2r[:, :], W2r),
                           (b1c[:, :], b1.rearrange("(p a) -> p a", a=1)),
                           (b2f[:, :], b2.rearrange("(a n) -> a n", a=1).broadcast_to([3, D]))):
                sp.dma_start(to, of).then_inc(s_w, 16)
            sp.wait_ge(s_fill, 4)
            att_flat, agg_flat = (t.rearrange("n w -> (n w)").rearrange("(c p f) -> c p f", c=ROUNDS, p=P)
                                  for t in (att_sums, agg_sums))
            with sp.Fori(0, ROUNDS) as c:
                sp.dma_start(att_flat[c], zeros).then_inc(s_z0, 16)
            with sp.Fori(0, ROUNDS - LEAD) as c:
                sp.wait_ge(h_ready, c + 1)
                sp.dma_start(agg_flat[c], zeros).then_inc(s_z1, 16)
            for c in range(ROUNDS - LEAD, ROUNDS):
                sp.dma_start(agg_flat[c], zeros).then_inc(s_z1, 16)
            sp.dma_start(out[N:TABLE, :].rearrange("(p r) w -> p (r w)", p=P), zeros[:, 0:(TABLE - N) * D // P]).then_inc(s_zo, 16)

            def load(k, c, whole, x_from, t_from):
                n = k % NB
                if whole:
                    sp.dma_start(xb[n][:].rearrange("p r w -> p (r w)"), x_from[0][c - 1]).then_inc(loaded[n], 16)
                    sp.dma_start(tb[n][:].rearrange("p r w -> p (r w)"), t_from[0][c - 1]).then_inc(loaded[n], 16)
                else:
                    sp.dma_start(xb[n][0:TAIL].rearrange("p r w -> p (r w)"), x_from[1]).then_inc(loaded[n], 16)
                    sp.dma_start(tb[n][0:TAIL].rearrange("p r w -> p (r w)"), t_from[1]).then_inc(loaded[n], 16)

            def stream(x_from, t_from, to, ready, per, before):
                load(0, 0, False, x_from, t_from)
                for i in range(1, NB - 1):
                    load(i, i, True, x_from, t_from)

                def body(i, k, g):
                    n = k % NB
                    if k + NB - 1 < ROUNDS:
                        if k:
                            sp.wait_ge(stored[(k - 1) % NB], (g + (k - 1) // NB + 1) * 16 + before[(k - 1) % NB])
                        load(k + NB - 1, i + NB - 1, True, x_from, t_from)
                    sp.wait_ge(ready, (i + 1) * per)
                    sp.dma_start(to[0][i - 1] if k else to[1], xb[n][0:P if k else TAIL].rearrange("p r w -> p (r w)")).then_inc(stored[n], 16)

                for i in range(PEEL):
                    body(i, i, 0)
                with sp.Fori(0, (ROUNDS - PEEL) // NB - 1) as g:
                    for k in range(PEEL, PEEL + NB):
                        body(g * NB + k, k, g)
                for i in range(ROUNDS - NB, ROUNDS):
                    body(i, i, 0)

            uses = [16 * len(range(n, ROUNDS, NB)) for n in range(NB)]
            sp.wait_ge(scattered, 64 * ROUNDS)
            stream((x_c, x_t), (att_c_, att_t), (x1_c, x1_t), x1_ready, 1, [0] * NB)
            for n in range(NB):
                sp.wait_ge(stored[n], uses[n])
            sp.wait_ge(scattered, 2 * 64 * ROUNDS)
            stream((x1_c, x1_t), (agg_c, agg_t), (out_c, out_t), y_read, 2, uses)
            for n in range(NB):
                sp.wait_ge(stored[n], 2 * uses[n])
            sp.wait_ge(s_zo, 16)

        @block.gpsimd
        def _(pool):
            G_ = nc.gpsimd
            G_.memset(src_key[:], PAD_KEY).then_inc(s_fill, 1)
            G_.memset(dst_key[:], PAD_KEY).then_inc(s_fill, 1)
            G_.memset(wqkv[:], 0.0).then_inc(s_fill, 1)
            G_.memset(zeros, 0.0).then_inc(s_fill, 1)
            G_.memset(ident[:], 0.0).then_inc(s_plain, 1)
            G_.memset(upto[:], 1.0).then_inc(s_plain, 1)
            G_.iota(spare[:], pattern=[[0, ROUNDS], [P, TILES]], base=N, channel_multiplier=1).then_inc(s_mask, 1)
            pool.wait_ge(s_plain, 2)
            G_.affine_select(out=ident[:], in_=ident[:], compare_op=ALU.not_equal, fill=1.0, base=0,
                             pattern=[[-1, P]], channel_multiplier=1).then_inc(s_mask, 1)
            G_.affine_select(out=upto[:, (TILES - 1) * P:], in_=upto[:, (TILES - 1) * P:], compare_op=ALU.is_ge, fill=0.0, base=0,
                             pattern=[[-1, P]], channel_multiplier=1).then_inc(s_mask, 1)

            def after_waits():
                pool.sem_inc(waits_met, 1)

            def gather(to, table, rows, c, s):
                pool.indirect_dma_start(out=to, out_offset=None, in_=table,
                                        in_offset=bass.IndirectOffsetOnAxis(ap=rows[:, c:c + 1], axis=0)).then_inc(s, 16)

            def scatter(b, k, table, of):
                pool.wait_ge(sums_ready, b + 1)
                pool.wait_ge(row_ready, b + 1)
                if k:
                    pool.wait_ge(scattered, 64 * b)
                after_waits()
                for j in range(TILES):
                    pool.indirect_dma_start(out=table, out_offset=bass.IndirectOffsetOnAxis(ap=sum_row[k % NB][:, j:j + 1], axis=0),
                                            in_=of[k % NB][:, j, :], in_offset=None, compute_op=ALU.add).then_inc(scattered, 16)

            def attention(i, k, g):
                pool.wait_ge(rx_ready, i + 1)
                if k >= NB:
                    pool.wait_ge(h_ready, i - NB + 1)
                    pool.wait_ge(kept_x, i - NB + 1)
                after_waits()
                for j in range(TILES):
                    for end in range(2):
                        gather(x_pair[k % NB][:, j, end, :], x, rows_x[k % NB], end * TILES + j, got_x[k % NB])
                if k == LEAD:
                    pool.wait_ge(s_z0, 16 * ROUNDS)
                if k >= LEAD:
                    scatter(i - LEAD, k - LEAD, att_sums, sums)

            rounds(pool, attention)
            for i in range(ROUNDS - LEAD, ROUNDS):
                scatter(i, i, att_sums, sums)

            pool.wait_ge(scattered, 64 * ROUNDS)
            pool.wait_ge(s_z1, 16 * ROUNDS)

            def sage(i, k, g):
                pool.wait_ge(ra_ready, i + 1)
                if k >= NB:
                    pool.wait_ge(he_ready, i - NB + 1)
                after_waits()
                for j in range(TILES):
                    gather(att_got[k % NB][:, j, :], att_sums, rows_att[k % NB], j, got_att[k % NB])
                if k >= LEAD:
                    scatter(i - LEAD + ROUNDS, k - LEAD + ROUNDS, agg_sums, sums)

            rounds(pool, sage)
            for i in range(2 * ROUNDS - LEAD, 2 * ROUNDS):
                scatter(i, i, agg_sums, sums)

            pool.wait_ge(scattered, 2 * 64 * ROUNDS)

            def messages(i, k, g):
                pool.wait_ge(rg_ready, i + 1)
                if k >= NB:
                    pool.wait_ge(agg_kept, i - NB + 1)
                after_waits()
                for j in range(2 * TILES):
                    gather(agg_got[k % NB][:, j, :], agg_sums, rows_agg[k % NB], j, got_agg[k % NB])

            rounds(pool, messages)

            for n in range(NB):
                pool.wait_ge(stored[n], 2 * 16 * len(range(n, ROUNDS, NB)))
            pool.wait_ge(s_zo, 16)
            rounds(pool, lambda i, k, g: scatter(i + 2 * ROUNDS, k + 2 * ROUNDS, out, sums_out))
            pool.wait_ge(scattered, 3 * 64 * ROUNDS)

        @block.vector
        def _(dve):
            chain = Chain(dve, v_step)
            link = chain.link

            V.memset(eps[:], EPS).then_inc(s_ones, 1)
            V.memset(ones3[:], 1.0).then_inc(s_ones, 1)
            V.memset(xb[0][:], 0.0).then_inc(s_ones, 1)
            V.memset(tb[0][:], 0.0).then_inc(s_ones, 1)
            for n in range(2):
                V.memset(h_e[n][:, :, D:W], 0.0).then_inc(s_ones, 1)
            dve.wait_ge(s_ones, 6)
            for n in range(2):
                V.memset(h_e[n][:, :, D:D + 1], 1.0).then_inc(s_ones, 1)
            dve.wait_ge(s_keys, 64)
            dve.wait_ge(s_mask, 3)
            V.memset(both_keys[:, ROUNDS:, :], 0)
            V.memset(x_rows[:, ROUNDS:, :], 0)
            for n, key in enumerate((src_key, dst_key)):
                one = slice(n * TILES, (n + 1) * TILES)
                half = keys_f[:, n * ROUNDS:(n + 1) * ROUNDS]
                V.tensor_copy(half[:, :, 0:TILES], key[:])
                V.tensor_tensor(half[:, :, TILES:], spare[:], key[:], ALU.subtract)
                V.tensor_scalar(x_rows[:, 0:ROUNDS, one], key[:], float(N - 1), None, ALU.min)
                link(V.tensor_copy(both_keys[:, 0:ROUNDS, one], key[:]))

            V.tensor_copy(keys_f[:, 2 * ROUNDS, :], keys_f[:, ROUNDS, :])
            dve.wait_ge(s_w, 16 * 9)
            link(V.tensor_copy(b2part[:, 0, :], b2f[:]))
            link(V.tensor_tensor(b2rest[:, 0, :], b2f[:], b2part[:, 0, :], ALU.subtract))
            link(V.tensor_copy(b2part[:, 1, :], b2rest[:, 0, :]))
            link(V.tensor_tensor(b2rest[:, 1, :], b2rest[:, 0, :], b2part[:, 1, :], ALU.subtract))
            link(V.tensor_copy(b2part[:, 2, :], b2rest[:, 1, :]))
            link(V.tensor_scalar(b2sel[:], b2part[:, 0, :], ident[0:3, 0:1], None, ALU.mult))
            for n in (1, 2):
                link(V.scalar_tensor_tensor(out=b2sel[:], in0=b2part[:, n, :], scalar=ident[0:3, n:n + 1], in1=b2sel[:],
                                            op0=ALU.mult, op1=ALU.add))
            V.tensor_copy(b2rows[:], b2sel[:].unsqueeze(1).broadcast_to([3, 8, D])).then_inc(s_b2, 1)

            def stage(rows, table, c, ready, width=2 * TILES):
                V.tensor_copy(rows[:], table[:, c, 0:width]).then_inc(ready, 1)

            def stage_first(rows, table, ready, width=2 * TILES):
                for n in range(LEAD):
                    stage(rows[n], table, n, ready, width)

            def stage_keys(k, slot):
                V.tensor_copy(key_col[k % 2][:], keys_f[:, slot, :]).then_inc(key_staged, 1)

            stage_first(rows_x, x_rows, rx_ready)
            stage_keys(0, 0)

            def compare(b, k, sums_only=False):
                dve.wait_ge(key_staged, b + 1)
                dve.wait_ge(key_rows, b + 1)
                if k >= 2:
                    dve.wait_ge(sum_done, b - 1)
                for j in range(TILES):
                    w = (j + 1) * P
                    if sums_only:
                        ins = V.tensor_scalar(same[k % 2][:, j, 0:w], key_row[k % 2][:, 0:w], key_col[k % 2][:, j:j + 1],
                                              None, ALU.is_equal)
                    else:
                        ins = V.scalar_tensor_tensor(out=same[k % 2][:, j, 0:w], in0=key_row[k % 2][:, 0:w],
                                                     scalar=key_col[k % 2][:, j:j + 1], in1=upto[:, (TILES - 1 - j) * P:],
                                                     op0=ALU.is_equal, op1=ALU.mult, accum_out=count[:, j:j + 1])
                ins.then_inc(same_done, 1)

            def target(b, k, keep=None):
                dve.wait_ge(same_done, b + 1)
                if k >= NB:
                    dve.wait_ge(scattered, 64 * (b - NB + 1))
                key = key_col[k % 2]
                link(V.scalar_tensor_tensor(out=pushed[:], in0=count[:], scalar=1.0, in1=key[:, TILES:], op0=ALU.is_gt, op1=ALU.mult))
                if keep is not None:
                    V.tensor_tensor(keep, pushed[:], key[:, 0:TILES], ALU.add)
                V.tensor_tensor(sum_row[k % NB][:], pushed[:], key[:, 0:TILES], ALU.add).then_inc(row_ready, 1)

            def statistics(of, n):
                for r in range(n):
                    ins = V.bn_stats(stats[:, r, :], of[:, r, :])
                link(ins)
                even, odd = stats[:, 0:n, 0:3], stats[:, 0:n, 3:6]
                V.tensor_tensor(mean2[:, 0:n], even[:, :, 1], odd[:, :, 1], ALU.add)
                V.tensor_tensor(ssq2[:, 0:n], even[:, :, 2], odd[:, :, 2], ALU.add)
                link(V.tensor_tensor(diff[:, 0:n], even[:, :, 1], odd[:, :, 1], ALU.subtract))
                link(V.scalar_tensor_tensor(out=diff[:, 0:n], in0=diff[:, 0:n], scalar=float(D // 4), in1=diff[:, 0:n], op0=ALU.mult, op1=ALU.mult))
                V.tensor_tensor(ssq[:, 0:n], ssq2[:, 0:n], diff[:, 0:n], ALU.add).then_inc(ssq_ready, 1)

            def normalise(of, to, middle, n, r):
                link(V.scalar_tensor_tensor(out=middle, in0=bcast(mean2[:, 0:n], D), scalar=-0.5, in1=of, op0=ALU.mult, op1=ALU.add))
                dve.wait_ge(rstd_ready, r + 1)
                return V.scalar_tensor_tensor(out=to, in0=middle, scalar=0.0, in1=bcast(rstd[:, 0:n], D), op0=ALU.max, op1=ALU.mult)

            def by_head(t):
                return t.rearrange("p t (h d) -> p t h d", h=HEADS)

            def scores(i, k):
                dve.wait_ge(qkv_done, i + 1)
                dve.wait_ge(q_copied, i + 1)
                link(V.tensor_tensor(qk[:].rearrange("p (a t) d -> p a t d", a=2), QKV[:, :, :, D:2 * D],
                                     q_sb[:].rearrange("p (a t) d -> p a t d", a=2), ALU.mult))
                link(V.reduce_sum(att[:], by_head(qk[:]), axis=AX.X))
                V.tensor_scalar(att_c[:], att[:], 10.0, -10.0, ALU.min, ALU.max).then_inc(att_ready, 1)

            def weighted(i, k):
                dve.wait_ge(exp_ready, i + 1)
                for a in range(2):
                    tiles = slice(2 * a, 2 * a + 2)
                    ins = V.tensor_tensor(by_head(vals[k % 2][:, tiles, 0:D]), by_head(QKV[:, a, :, 2 * D:3 * D]),
                                          bcast(vals[k % 2][:, tiles, D:W], HD), ALU.mult)
                ins.then_inc(vals_ready, 1)

            def attention(i, k, g):
                stage(rows_x[(k + LEAD) % NB], x_rows, i + LEAD, rx_ready)
                dve.wait_ge(got_x[k % NB], (g + k // NB + 1) * 128)
                pair = x_pair[k % NB].rearrange("p j e d -> p (j e) d")
                statistics(pair, 2 * TILES)
                stage_keys(k + 1, i + 1)
                compare(i, k)
                if k:
                    scores(i - 1, k - 1)
                normalise(pair, h_pair.rearrange("p j e d -> p (j e) d"), h_mid.rearrange("p j e d -> p (j e) d"),
                          2 * TILES, i).then_inc(h_ready, 1)
                if k:
                    weighted(i - 1, k - 1)
                target(i, k)

            rounds(dve, attention, chain, first=2)
            scores(ROUNDS - 1, ROUNDS - 1)
            weighted(ROUNDS - 1, ROUNDS - 1)

            stage_first(rows_att, both_keys, ra_ready, TILES)
            dve.wait_ge(kept_x, ROUNDS)

            def sage(i, k, g):
                n, b, kb = k % NB, i + ROUNDS, k + ROUNDS
                stage(rows_att[(k + LEAD) % NB], both_keys, i + LEAD, ra_ready, TILES)
                got, sums_n = att_got[n], tb[n]
                dve.wait_ge(got_att[n], (g + k // NB + 1) * 64)
                e_sum = chain.mark(V.tensor_scalar(z_inv[:], got[:, :, D:W], 1e-8, None, ALU.add))
                dve.wait_ge(loaded[n], (g + k // NB + 1) * 32)
                n_sum = chain.mark(V.tensor_scalar(zn[:], sums_n[:, :, D:W], 1e-8, None, ALU.add))
                chain.wait(e_sum)
                e_inv = chain.mark(V.reciprocal(z_inv[:], z_inv[:]))
                chain.wait(n_sum)
                n_inv = chain.mark(V.reciprocal(zn[:], zn[:]))
                chain.wait(e_inv)
                e_mul = chain.mark(V.tensor_tensor(by_head(x1_e[:]), by_head(got[:, :, 0:D]), bcast(z_inv[:], HD), ALU.mult))
                chain.wait(n_inv)
                n_mul = chain.mark(V.tensor_tensor(by_head(sums_n[:, :, 0:D]), by_head(sums_n[:, :, 0:D]), bcast(zn[:], HD), ALU.mult))
                chain.wait(e_mul)
                e_add = chain.mark(V.tensor_tensor(x1_e[:], x1_e[:], edge[:, bass.ts(i, TILES), :], ALU.add))
                chain.wait(n_mul)
                V.tensor_tensor(xb[n][:], xb[n][:], sums_n[:, :, 0:D], ALU.add).then_inc(x1_ready, 1)
                chain.wait(e_add)
                statistics(x1_e[:], TILES)
                stage_keys(kb + 1, b + 1)
                compare(b, kb)
                if k >= 2:
                    dve.wait_ge(kept_h, i - 1)
                normalise(x1_e[:], h_e[k % 2][:, :, 0:D], h_mid[:, :, 0, :], TILES, b).then_inc(he_ready, 1)
                target(b, kb, dst_row[:, i, :])

            rounds(dve, sage, chain)

            stage_first(rows_agg, both_keys, rg_ready)
            dve.wait_ge(sum_done, 2 * ROUNDS)
            dve.wait_ge(s_z1, 16 * ROUNDS)
            dve.wait_ge(s_zo, 16)

            def output(i, k):
                n = k % NB
                for half in range(2):
                    rows8 = slice(8 * half, 8 * half + 8)
                    dve.wait_ge(w2_done, i * 4 + 2 * half + 2)
                    V.tensor_tensor(xb[n][:, rows8, :], xb[n][:, rows8, :], Y[half].rearrange("p (r d) -> p r d", d=D),
                                    ALU.add).then_inc(y_read, 1)

            def nodes(i, k, g):
                u, n = k % 2, k % NB
                stage(rows_agg[(k + LEAD) % NB], both_keys, i + LEAD, rg_ready)
                dve.wait_ge(loaded[n], (g + k // NB + 1) * 32 + 32 * len(range(n, ROUNDS, NB)))
                statistics(xb[n][:], ROWS)
                link(V.tensor_scalar(inv_n[:], tb[n][:, :, D], 1.0, None, ALU.max))
                link(V.reciprocal(inv_n[:], inv_n[:]))
                if k >= 2:
                    dve.wait_ge(catT_done, i * 4 - 4)
                V.tensor_tensor(cat[u][:, :, 0, :], tb[n][:, :, 0:D], bcast(inv_n[:], D), ALU.mult)
                normalise(xb[n][:], cat[u][:, :, 1, :], mid, ROWS, i + 2 * ROUNDS).then_inc(cat_ready, 1)
                if k >= 2:
                    output(i - 2, k - 2)
                dve.wait_ge(got_agg[n], (g + k // NB + 1) * 128)
                link(V.tensor_scalar(inv_e[:], agg_got[n][:, :, D], 1.0, None, ALU.max))
                link(V.reciprocal(inv_e[:], inv_e[:]))
                V.tensor_copy(inv_dst[:, i, :], inv_e[:, TILES:])
                V.tensor_tensor(agg[:, bass.ts(i, TILES), :], agg_got[n][:, 0:TILES, 0:D], bcast(inv_e[:, 0:TILES], D),
                                ALU.mult).then_inc(agg_kept, 1)

            rounds(dve, nodes, chain)
            output(ROUNDS - 2, ROUNDS - 2)
            output(ROUNDS - 1, ROUNDS - 1)
            dve.wait_ge(agg_kept, ROUNDS)

            def means(i, k):
                if k >= 2:
                    dve.wait_ge(msgT_done, i - 1)
                V.tensor_copy(cat_e[k % 2][:, :, 0, :], agg[:, bass.ts(i, TILES), :]).then_inc(cat_e_agg, 1)

            def message(i, k):
                dve.wait_ge(w2l_done, i + 1)
                if k >= 2:
                    dve.wait_ge(sum_done, i - 1 + 2 * ROUNDS)
                V.tensor_tensor(msg[k % 2], MSG[k % 2][:, 0:TILES * D].rearrange("p (t d) -> p t d", d=D),
                                bcast(inv_dst[:, i, :], D), ALU.mult).then_inc(msg_ready, 1)

            means(0, 0)

            def last_sums(i, k, g):
                b, kb = i + 2 * ROUNDS, k + 2 * ROUNDS
                dve.wait_ge(same_done, b)
                stage_keys(kb + 1, i + ROUNDS + 1)
                dve.wait_ge(scattered, 64 * (b - NB + 1))
                V.tensor_copy(sum_row[kb % NB][:], dst_row[:, i, :]).then_inc(row_ready, 1)
                if k:
                    means(i, k)
                compare(b, kb, sums_only=True)
                if k:
                    message(i - 1, k - 1)

            rounds(dve, last_sums, chain)
            message(ROUNDS - 1, ROUNDS - 1)

        @block.scalar
        def _(act):
            chain = Chain(act, a_step)

            def copy_keys(b, k):
                act.wait_ge(keys_T, b + 1)
                if k >= 2:
                    act.wait_ge(same_done, b - 1)
                A.copy(key_row[k % 2][:], KEYS[:, :]).then_inc(key_rows, 1)

            def rsqrt(n, r):
                act.wait_ge(ssq_ready, r + 1)
                chain.link(A.activation(logv[:, 0:n], ssq[:, 0:n], ACT.Ln, bias=eps[:, 0:1], scale=1.0 / D))
                A.activation(rstd[:, 0:n], logv[:, 0:n], ACT.Exp, scale=-0.5).then_inc(rstd_ready, 1)

            def copy_sums(b, k, to, width):
                act.wait_ge(sum_done, b + 1)
                if k >= NB:
                    act.wait_ge(scattered, 64 * (b - NB + 1))
                A.copy(to[k % NB][:, :, :].rearrange("p t w -> p (t w)"), SUMS[k % 2][:, 0:TILES * width]).then_inc(sums_ready, 1)

            A.preload_act_table_set("natural_log_exp_and_others")
            act.wait_ge(s_ones, 8)
            act.wait_ge(s_w, 16 * 9)

            def q_and_exp(i, k):
                act.wait_ge(qkv_done, i + 1)
                if k:
                    act.wait_ge(att_ready, i)
                A.copy(q_sb[:].rearrange("p (a t) d -> p a t d", a=2), QKV[:, :, :, 0:D]).then_inc(q_copied, 1)
                act.wait_ge(att_ready, i + 1)
                if k >= 2:
                    act.wait_ge(sum_done, i - 1)
                A.activation(vals[k % 2][:, :, D:W], att_c[:], ACT.Exp).then_inc(exp_ready, 1)

            copy_keys(0, 0)

            def attention(i, k, g):
                act.wait_ge(got_x[k % NB], (g + k // NB + 1) * 128)
                A.copy(edge[:, bass.ts(i, TILES), :], x_pair[k % NB][:, :, 0, :]).then_inc(kept_x, 1)
                rsqrt(2 * TILES, i)
                if k:
                    q_and_exp(i - 1, k - 1)
                act.wait_ge(hT_done, i + 1)
                A.copy(hT[:], HT[:, :]).then_inc(hT_copied, 1)
                if k:
                    copy_sums(i - 1, k - 1, sums, W)
                copy_keys(i + 1, k + 1)

            rounds(act, attention, chain)
            q_and_exp(ROUNDS - 1, ROUNDS - 1)
            copy_sums(ROUNDS - 1, ROUNDS - 1, sums, W)

            def sage(i, k, g):
                b, kb = i + ROUNDS, k + ROUNDS
                rsqrt(TILES, b)
                act.wait_ge(he_ready, i + 1)
                A.copy(edge[:, bass.ts(i, TILES), :], h_e[k % 2][:, :, 0:D]).then_inc(kept_h, 1)
                copy_keys(b + 1, kb + 1)
                copy_sums(b, kb, sums, W)

            rounds(act, sage, chain)
            act.wait_ge(kept_h, ROUNDS)

            def group(i, k, q):
                n, kn = i * 4 + q, k * 4 + q
                act.wait_ge(catT_done, n + 1)
                if kn >= 2:
                    act.wait_ge(g_done, n - 1)
                A.copy(catT[kn % 2][:], CATT[:, kn % 2, :]).then_inc(catT_copied, 1)
                if kn:
                    relu(n - 1, kn - 1)

            def relu(n, kn):
                act.wait_ge(g_done, n + 1)
                if kn >= 2:
                    act.wait_ge(w2_done, n - 1)
                A.activation(gT[kn % 2][:], G[kn % 2], ACT.Relu, bias=b1c[:, 0:1]).then_inc(g_ready, 1)

            def nodes(i, k, g):
                if k:
                    group(i - 1, k - 1, 0)
                    group(i - 1, k - 1, 1)
                rsqrt(ROWS, i + 2 * ROUNDS)
                if k:
                    group(i - 1, k - 1, 2)
                    group(i - 1, k - 1, 3)

            rounds(act, nodes, chain)
            for q in range(4):
                group(ROUNDS - 1, ROUNDS - 1, q)
            relu(4 * ROUNDS - 1, 4 * ROUNDS - 1)

            def edge_h(i, k):
                if k >= 2:
                    act.wait_ge(msgT_done, i - 1)
                A.copy(cat_e[k % 2][:, :, 1, :], edge[:, bass.ts(i, TILES), :]).then_inc(cat_e_h, 1)

            def edge_group(i, k):
                act.wait_ge(msgT_done, i + 1)
                if k:
                    act.wait_ge(eg_done, i)
                A.copy(catT[0][:], CATT[:, 0, :]).then_inc(msgT_copied, 1)

            def edge_relu(i, k):
                act.wait_ge(eg_done, i + 1)
                if k:
                    act.wait_ge(w2l_done, i)
                A.activation(gT[0][:], G[0], ACT.Relu, bias=b1c[:, 0:1]).then_inc(eg_ready, 1)

            act.wait_ge(w2_done, 4 * ROUNDS)
            edge_h(0, 0)

            def last_sums(i, k, g):
                b, kb = i + 2 * ROUNDS, k + 2 * ROUNDS
                if k:
                    edge_h(i, k)
                edge_group(i, k)
                if k:
                    copy_sums(b - 1, kb - 1, sums_out, D)
                edge_relu(i, k)
                copy_keys(b + 1, kb + 1)

            rounds(act, last_sums, chain)
            copy_sums(3 * ROUNDS - 1, 3 * ROUNDS - 1, sums_out, D)

        @block.tensor
        def _(pe):
            def transpose_keys(b, k):
                pe.wait_ge(key_staged, b + 1)
                if k:
                    pe.wait_ge(key_rows, b)
                for j in range(TILES):
                    ins = T.transpose(KEYS[:, j * P:(j + 1) * P], key_col[k % 2][:, j:j + 1].broadcast_to([P, P]), ident[:])
                ins.then_inc(keys_T, 1)

            def sum_up(b, k, values, width):
                pe.wait_ge(same_done, b + 1)
                if k >= 2:
                    pe.wait_ge(sums_ready, b - 1)
                for i in range(TILES):
                    for j in range(i, TILES):
                        ins = T.matmul(SUMS[k % 2][:, i * width:(i + 1) * width], same[k % 2][:, j, i * P:(i + 1) * P],
                                       values(j), start=(j == i), stop=(j == TILES - 1))
                ins.then_inc(sum_done, 1)

            pe.wait_ge(s_mask, 3)
            pe.wait_ge(s_ones, 8)
            pe.wait_ge(s_w, 16 * 9)

            transpose_keys(0, 0)

            def sum_attention(i, k):
                pe.wait_ge(vals_ready, i + 1)
                sum_up(i, k, lambda j: vals[k % 2][:, j, :], W)

            def attention(i, k, g):
                pe.wait_ge(h_ready, i + 1)
                if k:
                    pe.wait_ge(hT_copied, i)
                for j in range(TILES):
                    ins = T.transpose(HT[:, j * P:(j + 1) * P], h_pair[:, j].rearrange("p e d -> p (e d)"), ident[:])
                ins.then_inc(hT_done, 1)
                if k:
                    sum_attention(i - 1, k - 1)
                transpose_keys(i + 1, k + 1)
                pe.wait_ge(hT_copied, i + 1)
                for j in range(TILES):
                    ins = T.matmul(QKV[:, j // 2, j % 2, :], hT[:, j * P:(j + 1) * P], wqkv[:], start=True, stop=True)
                ins.then_inc(qkv_done, 1)

            rounds(pe, attention)
            sum_attention(ROUNDS - 1, ROUNDS - 1)

            def sage(i, k, g):
                b, kb = i + ROUNDS, k + ROUNDS
                transpose_keys(b + 1, kb + 1)
                pe.wait_ge(he_ready, i + 1)
                sum_up(b, kb, lambda j: h_e[k % 2][:, j, :], W)

            rounds(pe, sage)

            pe.wait_ge(sums_ready, 2 * ROUNDS)
            pe.wait_ge(s_b2, 1)

            def times_w1(n, kn):
                pe.wait_ge(catT_copied, n + 1)
                if kn >= 2:
                    pe.wait_ge(g_ready, n - 1)
                T.matmul(G[kn % 2], w1[:], catT[kn % 2][:], start=True, stop=True).then_inc(g_done, 1)

            def times_w2(i, k, q):
                n, kn = i * 4 + q, k * 4 + q
                pe.wait_ge(g_ready, n + 1)
                half = q // 2
                if q % 2 == 0:
                    if k:
                        pe.wait_ge(y_read, i * 2 + half - 1)
                    T.matmul(Y[half], ones3[:], b2rows[:].rearrange("p a d -> p (a d)"), start=True, stop=False)
                for t in range(4):
                    at = (q % 2 * 4 + t) * D
                    ins = T.matmul(Y[half][:, at:at + D], gT[kn % 2][:, t * P:(t + 1) * P], w2r[:], start=False,
                                   stop=(q % 2 == 1 and t == 3))
                ins.then_inc(w2_done, 1)

            def nodes(i, k, g):
                for q in range(4):
                    n, kn = i * 4 + q, k * 4 + q
                    if q == 0:
                        pe.wait_ge(cat_ready, i + 1)
                    if kn >= 2:
                        pe.wait_ge(catT_copied, n - 1)
                    for t in range(4):
                        ins = T.transpose(CATT[:, kn % 2, t * P:(t + 1) * P], cat[k % 2][:, 4 * q + t].rearrange("p e d -> p (e d)"), ident[:])
                    ins.then_inc(catT_done, 1)
                    if kn >= 1:
                        times_w1(n - 1, kn - 1)
                    if kn >= 2:
                        if q >= 2:
                            times_w2(i, k, q - 2)
                        else:
                            times_w2(i - 1, k - 1, q + 2)

            rounds(pe, nodes)
            times_w1(4 * ROUNDS - 1, 4 * ROUNDS - 1)
            times_w2(ROUNDS - 1, ROUNDS - 1, 2)
            times_w2(ROUNDS - 1, ROUNDS - 1, 3)

            pe.wait_ge(y_read, 2 * ROUNDS)

            def edge_transposes(i, k):
                pe.wait_ge(cat_e_agg, i + 1)
                pe.wait_ge(cat_e_h, i + 1)
                if k:
                    pe.wait_ge(msgT_copied, i)
                for t in range(TILES):
                    ins = T.transpose(CATT[:, 0, t * P:(t + 1) * P], cat_e[k % 2][:, t].rearrange("p e d -> p (e d)"), ident[:])
                ins.then_inc(msgT_done, 1)

            def edge_w1(i, k):
                pe.wait_ge(msgT_copied, i + 1)
                if k:
                    pe.wait_ge(eg_ready, i)
                T.matmul(G[0], w1[:], catT[0][:], start=True, stop=True).then_inc(eg_done, 1)

            def edge_w2(i, k):
                pe.wait_ge(eg_ready, i + 1)
                if k >= 2:
                    pe.wait_ge(msg_ready, i - 1)
                for t in range(TILES):
                    ins = T.matmul(MSG[k % 2][:, t * D:(t + 1) * D], gT[0][:, t * P:(t + 1) * P], w2l[:], start=True, stop=True)
                ins.then_inc(w2l_done, 1)

            def sum_messages(i, k):
                b, kb = i + 2 * ROUNDS, k + 2 * ROUNDS
                pe.wait_ge(msg_ready, i + 1)
                sum_up(b, kb, lambda j: msg[k % 2][:, j, :], D)

            def last_sums(i, k, g):
                edge_transposes(i, k)
                if k:
                    sum_messages(i - 1, k - 1)
                edge_w1(i, k)
                transpose_keys(i + 2 * ROUNDS + 1, k + 2 * ROUNDS + 1)
                edge_w2(i, k)

            rounds(pe, last_sums)
            sum_messages(ROUNDS - 1, ROUNDS - 1)


_INS = ["x", "src", "dst", "L0_gnn_Wq", "L0_gnn_Wk", "L0_gnn_Wv", "L1_gnn_W1l", "L1_gnn_b1", "L1_gnn_W1r",
        "L1_gnn_W2l", "L1_gnn_b2", "L1_gnn_W2r"]


def kernel(**inputs):
    import numpy as np
    import concourse.bacc as bacc
    from concourse.bass_utils import run_bass_kernel_spmd

    nc = bacc.Bacc("TRN2", target_bir_lowering=False, num_devices=1)
    arrays, args = {}, []
    for name in _INS:
        a = np.ascontiguousarray(inputs[name])
        arrays[f"in_{name}"] = a
        args.append(nc.dram_tensor(f"in_{name}", a.shape, mybir.dt.from_np(a.dtype), kind="ExternalInput").ap())
    out = nc.dram_tensor("out", (TABLE, D), mybir.dt.float32, kind="ExternalOutput").ap()
    gnn_kernel(nc, *args, out)
    r = run_bass_kernel_spmd(nc, [arrays], core_ids=[0])
    return r.results[0]["out"][0:N]
```

```python
import concourse.bass as bass
from concourse import mybir
from contextlib import ExitStack

N, E, D, HEADS, HID = 100000, 25000, 64, 4, 128
HD = D // HEADS
P = 128
COLS = -(-E // P)
TILES = 4
ROUNDS = COLS // TILES
W = D + HEADS
PAD_KEY = N + TILES * P
TABLE = -(-(PAD_KEY + 1) // (ROUNDS * P // 4)) * (ROUNDS * P // 4)
ROWS = 16
CHUNK = P * ROWS
FULL = N // CHUNK
TAIL = (N - FULL * CHUNK) // ROWS
NB = 4
LEAD = 3
PEEL = 5
EARLY = range(NB, 2 * NB + 1)
LATE = 3 * NB
EPS = 1e-5
assert COLS == ROUNDS * TILES and FULL + 1 == ROUNDS and FULL * CHUNK + TAIL * ROWS == N
assert (ROUNDS - PEEL) % NB == 0 == (ROUNDS - EARLY.stop) % NB and TABLE * W % (ROUNDS * P) == 0
ZW = TABLE * W // (ROUNDS * P)


class Chain:

    def __init__(self, eng, sem):
        self.eng, self.sem, self.n, self.g = eng, sem, 0, None

    def link(self, ins):
        self.wait(self.mark(ins))

    def mark(self, ins):
        ins.then_inc(self.sem, 1)
        self.n += 1
        return self.n

    def wait(self, n):
        self.eng.wait_ge(self.sem, n if self.g is None else self.g + n)


def rounds(eng, body, chain=None, first=0, peel=PEEL, done=0):
    start = chain.n - first if chain else 0
    for i in range(done, peel):
        body(i, i, 0)
    per = (chain.n - start) // peel if chain else 0
    with eng.Fori(0, (ROUNDS - peel) // NB) as g:
        for k in range(peel, peel + NB):
            if chain:
                chain.g, chain.n = g * (per * NB), start + per * k
            body(g * NB + k, k, g)
            if chain:
                assert chain.n == start + per * (k + 1)
    if chain:
        chain.g, chain.n = None, start + per * ROUNDS


def gnn_kernel(nc, x, src, dst, Wq, Wk, Wv, W1l, b1, W1r, W2l, b2, W2r, out):
    fp32, bf16, i32 = mybir.dt.float32, mybir.dt.bfloat16, mybir.dt.int32
    ALU, ACT, AX = mybir.AluOpType, mybir.ActivationFunctionType, mybir.AxisListType
    V, A, T = nc.vector, nc.scalar, nc.tensor

    ctx = ExitStack()
    with ctx:
        def sb(name, shape, dt=fp32):
            return ctx.enter_context(nc.sbuf_tensor(name, shape, dt))

        def pb(name, shape, dt=fp32):
            return ctx.enter_context(nc.psum_tensor(name, shape, dt))

        def sem(name):
            return ctx.enter_context(nc.semaphore(name))

        def two(make, name, *shape):
            return [make(f"{name}{n}", *shape) for n in range(2)]

        def ring(make, name, *shape):
            return [make(f"{name}{n}", *shape) for n in range(NB)]

        att_sums = nc.dram_tensor("att_sums", [TABLE, W], fp32).ap()
        agg_sums = nc.dram_tensor("agg_sums", [TABLE, W], fp32).ap()
        x1_dram = nc.dram_tensor("x1_dram", [N, D], fp32).ap()

        ident = sb("ident", [P, P])
        upto = sb("upto", [P, TILES * P])
        work = sb("work", [P, ZW])
        zeros = work[:, :]
        mid = work[:, 0:ROWS * D].rearrange("p (r d) -> p r d", d=D)
        eps = sb("eps", [P, 1])
        wqkv = sb("wqkv", [P, 3 * D])
        w1 = sb("w1", [P, HID])
        w2l = sb("w2l", [P, D])
        w2r = sb("w2r", [P, D])
        b1c = sb("b1c", [P, 1])
        b2f = sb("b2f", [3, D])
        b2part = sb("b2part", [3, 3, D], bf16)
        b2rest = sb("b2rest", [3, 2, D])
        b2sel = sb("b2sel", [3, D])
        b2rows = sb("b2rows", [3, 8, D], bf16)
        ones3 = sb("ones3", [3, P], bf16)

        src_key = sb("src_key", [P, ROUNDS, TILES], i32)
        dst_key = sb("dst_key", [P, ROUNDS, TILES], i32)
        spare = sb("spare", [P, ROUNDS, TILES], i32)
        both_keys = sb("both_keys", [P, ROUNDS + LEAD, 2 * TILES], i32)
        x_rows = sb("x_rows", [P, ROUNDS + LEAD, 2 * TILES], i32)
        keys_f = sb("keys_f", [P, 2 * ROUNDS + 1, 2 * TILES])
        dst_row = sb("dst_row", [P, ROUNDS, TILES], i32)
        edge = sb("edge", [P, COLS, D])
        agg = sb("agg", [P, COLS, D])
        inv = sb("inv", [P, ROUNDS, 2 * TILES])

        key_col = two(sb, "key_col", [P, 2 * TILES])
        key_row = two(sb, "key_row", [P, TILES * P])
        same = two(sb, "same", [P, TILES, TILES * P])
        count = sb("count", [P, TILES])
        pushed = sb("pushed", [P, TILES])
        sums = ring(sb, "sums", [P, TILES, W])
        sums_out = [s[:].rearrange("p t w -> p (t w)")[:, 0:TILES * D].rearrange("p (t d) -> p t d", d=D) for s in sums]
        sum_row = ring(sb, "sum_row", [P, TILES], i32)

        stats = sb("stats", [P, ROWS, 6])
        mean2 = sb("mean2", [P, ROWS])
        diff = sb("diff", [P, ROWS])
        ssq = sb("ssq", [P, ROWS])
        ssq2 = sb("ssq2", [P, ROWS])
        logv = sb("logv", [P, ROWS])
        rstd = sb("rstd", [P, ROWS])

        rows_x = ring(sb, "rows_x", [P, 2 * TILES], i32)
        rows_att = ring(sb, "rows_att", [P, TILES], i32)
        rows_agg = ring(sb, "rows_agg", [P, 2 * TILES], i32)
        agg_got = ring(sb, "agg_got", [P, 2 * TILES, W])
        x_pair = [t[:].rearrange("p j w -> p (j w)")[:, 0:TILES * 2 * D].rearrange("p (j e d) -> p j e d", e=2, d=D) for t in agg_got]
        att_got = [t[:, 0:TILES, :] for t in agg_got]
        x_early = [agg[:, bass.ts(n, 2 * TILES), :].rearrange("p (j e) d -> p j e d", e=2) for n in range(len(EARLY))]

        catT = two(sb, "catT", [P, 4 * P])
        gT = two(sb, "gT", [P, 4 * P])
        h_mid, h_pair = (t[:].rearrange("p (j e d) -> p j e d", e=2, d=D) for t in gT)
        x_mid = [t[:, :, 0, :] for t in (h_mid, h_pair)]
        hT = catT[0]
        q_sb = sb("q_sb", [P, TILES, D])
        qk = sb("qk", [P, TILES, D])
        att = sb("att", [P, TILES, HEADS])
        att_c = sb("att_c", [P, TILES, HEADS])
        vals = two(sb, "vals", [P, TILES, W])
        z_inv = sb("z_inv", [P, TILES, HEADS])
        x1_e = sb("x1_e", [P, TILES, D])
        h_e = two(sb, "h_e", [P, TILES, W])
        msg = [t[:].rearrange("p t w -> p (t w)")[:, 0:TILES * D].rearrange("p (t d) -> p t d", d=D) for t in vals]

        xb = [sb(f"xb{n}", [P, ROWS, D]) for n in range(NB)]
        tb = [sb(f"tb{n}", [P, ROWS, W]) for n in range(NB)]
        cat_e = [t[:].rearrange("p r w -> p (r w)")[:, 0:TILES * 2 * D].rearrange("p (j e d) -> p j e d", e=2, d=D) for t in tb[0:2]]
        zn = sb("zn", [P, ROWS, HEADS])
        cat = [same[n][:].rearrange("p j (r e d) -> p (j r) e d", e=2, d=D) for n in range(2)]
        inv_n = sb("inv_n", [P, ROWS])

        bank = pb("bank", [P, 8, 512])
        KEYS, HT, SUMS = bank[:, 0, :], bank[:, 1, :], [bank[:, 4, :], bank[:, 5, :]]
        QKV = bank[:, 2:4, 0:6 * D].rearrange("p a (t w) -> p a t w", t=2)
        CATT, G = bank[:, 2:4, :], [bank[:, 1, :], bank[:, 6, :]]
        Y = [[bank[:, 7, :], bank[:, 5, :]], [bank[:, 0, :], bank[:, 4, :]]]
        MSG = [bank[:, 6, :], bank[:, 7, :]]

        s_w, s_keys = sem("weights_in"), sem("edges_in")
        s_fill, s_mask, s_ones = sem("filled"), sem("masks_made"), sem("constants_set")
        s_plain = sem("masks_filled")
        s_z0, s_z1, s_zo = sem("att_sums_zeroed"), sem("agg_sums_zeroed"), sem("spare_rows_zeroed")
        x_rows_ready = sem("x_rows_ready")
        s_b2 = sem("b2_ready")
        v_step, a_step = sem("vector_step"), sem("scalar_step")
        key_staged, keys_T, key_rows = sem("key_staged"), sem("keys_transposed"), sem("key_rows_copied")
        same_done, sum_done = sem("same_done"), sem("sum_done")
        sums_ready, row_ready = sem("sums_ready"), sem("sum_row_ready")
        scattered = sem("scattered")
        waits_met = sem("waits_met")
        rx_ready, ra_ready, rg_ready = sem("rows_x_ready"), sem("rows_att_ready"), sem("rows_agg_ready")
        got_early = [sem(f"got_x_early{n}") for n in range(len(EARLY))]
        got_x, got_att, got_agg = ring(sem, "got_x"), ring(sem, "got_att"), ring(sem, "got_agg")
        ssq_ready, rstd_ready = sem("ssq_ready"), sem("rstd_ready")
        h_ready, hT_done, hT_copied = sem("h_ready"), sem("hT_done"), sem("hT_copied")
        qkv_done, q_copied, att_ready, exp_ready = sem("qkv_done"), sem("q_copied"), sem("att_ready"), sem("exp_ready")
        vals_ready, kept_x, kept_h = sem("vals_ready"), sem("kept_x"), sem("kept_h")
        xm_ready, he_ready = sem("x_centred"), sem("h_edge_ready")
        loaded = [sem(f"chunk_loaded{n}") for n in range(NB)]
        stored = [sem(f"chunk_stored{n}") for n in range(NB)]
        x1_ready = sem("x1_ready")
        cat_ready, cat_e_agg, cat_e_h = sem("cat_ready"), sem("cat_e_agg_ready"), sem("cat_e_h_ready")
        catT_done, catT_copied, g_done, g_ready = sem("catT_done"), sem("catT_copied"), sem("g_done"), sem("g_ready")
        w2_done = sem("w2_done")
        y_read, msg_ready, agg_kept = sem("y_read"), sem("messages_ready"), sem("agg_kept")
        msgT_done, msgT_copied = sem("edge_catT_done"), sem("edge_catT_copied")
        eg_done, eg_ready, w2l_done = sem("edge_g_done"), sem("edge_g_ready"), sem("w2l_done")

        def chunk_of(t, width):
            return t[0:FULL * CHUNK, :].rearrange("(c p r) w -> c p (r w)", p=P, r=ROWS), \
                t[FULL * CHUNK:N, :].rearrange("(p r) w -> p (r w)", r=ROWS)

        x_chunks, x_t = chunk_of(x, D)
        att_chunks, att_t = chunk_of(att_sums, W)
        agg_chunks, agg_t = chunk_of(agg_sums, W)
        x1_chunks, x1_t = chunk_of(x1_dram, D)
        out_chunks, out_t = chunk_of(out, D)

        def bcast(col, inner):
            return col.unsqueeze(len(col.shape)).broadcast_to([*col.shape, inner])

        def pair_of(k, g):
            if k in EARLY:
                return x_early[k - NB], got_early[k - NB], 128
            elsewhere = len([e for e in EARLY if e < k and e % NB == k % NB])
            return x_pair[k % NB], got_x[k % NB], (g + k // NB + 1 - elsewhere) * 128

        block = ctx.enter_context(nc.Block())

        @block.sync
        def _(sp):
            last = E - (P - 1) * COLS
            for key, given in ((src_key, src), (dst_key, dst)):
                flat = key[:].rearrange("p a b -> p (a b)")
                if key is src_key:
                    sp.wait_ge(s_fill, 2)
                sp.dma_start(flat[0:P - 1, :], given[0:(P - 1) * COLS].rearrange("(p c) -> p c", c=COLS)).then_inc(s_keys, 16)
                sp.dma_start(flat[P - 1:P, 0:last], given[(P - 1) * COLS:E].rearrange("(p c) -> p c", p=1)).then_inc(s_keys, 16)
            sp.wait_ge(s_fill, 3)
            for to, of in ((wqkv[0:D, 0:D], Wq), (wqkv[D:P, D:2 * D], Wk), (wqkv[D:P, 2 * D:3 * D], Wv),
                           (w1[0:D, :], W1l), (w1[D:P, :], W1r), (w2l[:, :], W2l), (w2r[:, :], W2r),
                           (b1c[:, :], b1.rearrange("(p a) -> p a", a=1)),
                           (b2f[:, :], b2.rearrange("(a n) -> a n", a=1).broadcast_to([3, D]))):
                sp.dma_start(to, of).then_inc(s_w, 16)
            sp.wait_ge(s_fill, 4)
            att_flat, agg_flat = (t.rearrange("n w -> (n w)").rearrange("(c p f) -> c p f", c=ROUNDS, p=P)
                                  for t in (att_sums, agg_sums))
            with sp.Fori(0, ROUNDS) as c:
                sp.dma_start(att_flat[c], zeros).then_inc(s_z0, 16)
            with sp.Fori(0, ROUNDS - LEAD) as c:
                sp.wait_ge(h_ready, c + 1)
                sp.dma_start(agg_flat[c], zeros).then_inc(s_z1, 16)
            for c in range(ROUNDS - LEAD, ROUNDS):
                sp.dma_start(agg_flat[c], zeros).then_inc(s_z1, 16)
            sp.dma_start(out[N:TABLE, :].rearrange("(p r) w -> p (r w)", p=P), zeros[:, 0:(TABLE - N) * D // P]).then_inc(s_zo, 16)

            def load_x(k, c, whole, x_from):
                n = k % NB
                rows = xb[n][0:P if whole else TAIL].rearrange("p r w -> p (r w)")
                sp.dma_start(rows, x_from[0][c - 1] if whole else x_from[1]).then_inc(loaded[n], 16)

            def load_sums(k, c, whole, t_from):
                n = k % NB
                rows = tb[n][0:P if whole else TAIL].rearrange("p r w -> p (r w)")
                sp.dma_start(rows, t_from[0][c - 1] if whole else t_from[1]).then_inc(loaded[n], 16)

            def stream(x_from, t_from, to, ready, per, before, batches):
                for i in range(NB - 1):
                    load_x(i, i, i > 0, x_from)
                sp.wait_ge(scattered, 64 * batches)
                for i in range(NB - 1):
                    load_sums(i, i, i > 0, t_from)

                def body(i, k, g):
                    n = k % NB
                    if k + NB - 1 < ROUNDS:
                        if k:
                            sp.wait_ge(stored[(k - 1) % NB], (g + (k - 1) // NB + 1) * 16 + before[(k - 1) % NB])
                        load_x(k + NB - 1, i + NB - 1, True, x_from)
                        load_sums(k + NB - 1, i + NB - 1, True, t_from)
                    sp.wait_ge(ready, (i + 1) * per)
                    sp.dma_start(to[0][i - 1] if k else to[1], xb[n][0:P if k else TAIL].rearrange("p r w -> p (r w)")).then_inc(stored[n], 16)

                for i in range(PEEL):
                    body(i, i, 0)
                with sp.Fori(0, (ROUNDS - PEEL) // NB - 1) as g:
                    for k in range(PEEL, PEEL + NB):
                        body(g * NB + k, k, g)
                for i in range(ROUNDS - NB, ROUNDS):
                    body(i, i, 0)

            uses = [16 * len(range(n, ROUNDS, NB)) for n in range(NB)]
            sp.wait_ge(s_ones, 8)
            stream((x_chunks, x_t), (att_chunks, att_t), (x1_chunks, x1_t), x1_ready, 1, [0] * NB, ROUNDS)
            for n in range(NB):
                sp.wait_ge(stored[n], uses[n])
            stream((x1_chunks, x1_t), (agg_chunks, agg_t), (out_chunks, out_t), y_read, 2, uses, 2 * ROUNDS)
            for n in range(NB):
                sp.wait_ge(stored[n], 2 * uses[n])
            sp.wait_ge(s_zo, 16)

        @block.gpsimd
        def _(pool):
            G_ = nc.gpsimd
            G_.memset(src_key[:], PAD_KEY).then_inc(s_fill, 1)
            G_.memset(dst_key[:], PAD_KEY).then_inc(s_fill, 1)
            G_.memset(wqkv[:], 0.0).then_inc(s_fill, 1)
            G_.memset(zeros, 0.0).then_inc(s_fill, 1)
            G_.memset(ident[:], 0.0).then_inc(s_plain, 1)
            G_.memset(upto[:], 1.0).then_inc(s_plain, 1)
            G_.iota(spare[:], pattern=[[0, ROUNDS], [P, TILES]], base=N, channel_multiplier=1).then_inc(s_mask, 1)
            pool.wait_ge(s_plain, 2)
            G_.affine_select(out=ident[:], in_=ident[:], compare_op=ALU.not_equal, fill=1.0, base=0,
                             pattern=[[-1, P]], channel_multiplier=1).then_inc(s_mask, 1)
            G_.affine_select(out=upto[:, (TILES - 1) * P:], in_=upto[:, (TILES - 1) * P:], compare_op=ALU.is_ge, fill=0.0, base=0,
                             pattern=[[-1, P]], channel_multiplier=1).then_inc(s_mask, 1)

            def after_waits():
                pool.sem_inc(waits_met, 1)

            def gather(to, table, rows, c, s):
                pool.indirect_dma_start(out=to, out_offset=None, in_=table,
                                        in_offset=bass.IndirectOffsetOnAxis(ap=rows[:, c:c + 1], axis=0)).then_inc(s, 16)

            def scatter(b, k, table, of):
                pool.wait_ge(sums_ready, b + 1)
                pool.wait_ge(row_ready, b + 1)
                if k:
                    pool.wait_ge(scattered, 64 * b)
                after_waits()
                for j in range(TILES):
                    pool.indirect_dma_start(out=table, out_offset=bass.IndirectOffsetOnAxis(ap=sum_row[k % NB][:, j:j + 1], axis=0),
                                            in_=of[k % NB][:, j, :], in_offset=None, compute_op=ALU.add).then_inc(scattered, 16)

            def gather_x(k, rows, those=range(2 * TILES)):
                to, got, _ = pair_of(k, 0)
                for n in those:
                    j, end = n // 2, n % 2
                    gather(to[:, j, end, :], x, rows, end * TILES + j, got)

            pool.wait_ge(x_rows_ready, 2)
            for k in range(EARLY.stop):
                gather_x(k, x_rows[:, k, :])
            pool.wait_ge(h_ready, NB)
            pool.wait_ge(kept_x, NB)
            gather_x(EARLY.stop, x_rows[:, EARLY.stop, :])
            pool.wait_ge(s_z0, 16 * ROUNDS)
            scatter(0, 0, att_sums, sums)
            done = 1
            for k in range(EARLY.stop + 1, LATE + 1):
                if k == LATE:
                    pool.wait_ge(rx_ready, 1)
                for those in (range(0, 3), range(3, 6), range(6, 8)):
                    after_waits()
                    gather_x(k, x_rows[:, k, :] if k < LATE else rows_x[k % NB], those)
                    scatter(done, done, att_sums, sums)
                    done += 1
            assert done == LATE + 1 - LEAD

            def attention(i, k, g):
                pool.wait_ge(rx_ready, i - LATE + 1)
                pool.wait_ge(h_ready, i - NB + 1)
                pool.wait_ge(kept_x, i - NB + 1)
                after_waits()
                gather_x(k, rows_x[k % NB])
                scatter(i - LEAD, k - LEAD, att_sums, sums)

            rounds(pool, attention, peel=LATE + 1, done=LATE + 1)
            for i in range(ROUNDS - LEAD, ROUNDS):
                scatter(i, i, att_sums, sums)

            pool.wait_ge(scattered, 64 * ROUNDS)
            pool.wait_ge(s_z1, 16 * ROUNDS)

            def sage(i, k, g):
                pool.wait_ge(ra_ready, i + 1)
                if k >= NB:
                    pool.wait_ge(he_ready, i - NB + 1)
                after_waits()
                for j in range(TILES):
                    gather(att_got[k % NB][:, j, :], att_sums, rows_att[k % NB], j, got_att[k % NB])
                if k >= LEAD:
                    scatter(i - LEAD + ROUNDS, k - LEAD + ROUNDS, agg_sums, sums)

            rounds(pool, sage)
            for i in range(2 * ROUNDS - LEAD, 2 * ROUNDS):
                scatter(i, i, agg_sums, sums)

            pool.wait_ge(scattered, 2 * 64 * ROUNDS)

            def messages(i, k, g):
                pool.wait_ge(rg_ready, i + 1)
                if k >= NB:
                    pool.wait_ge(agg_kept, i - NB + 1)
                after_waits()
                for j in range(2 * TILES):
                    gather(agg_got[k % NB][:, j, :], agg_sums, rows_agg[k % NB], j, got_agg[k % NB])

            rounds(pool, messages)

            for n in range(NB):
                pool.wait_ge(stored[n], 2 * 16 * len(range(n, ROUNDS, NB)))
            pool.wait_ge(s_zo, 16)
            rounds(pool, lambda i, k, g: scatter(i + 2 * ROUNDS, k + 2 * ROUNDS, out, sums_out))
            pool.wait_ge(scattered, 3 * 64 * ROUNDS)

        @block.vector
        def _(dve):
            chain = Chain(dve, v_step)
            link = chain.link

            V.memset(eps[:], EPS).then_inc(s_ones, 1)
            V.memset(ones3[:], 1.0).then_inc(s_ones, 1)
            V.memset(xb[0][:], 0.0).then_inc(s_ones, 1)
            V.memset(tb[0][:], 0.0).then_inc(s_ones, 1)
            for n in range(2):
                V.memset(h_e[n][:, :, D:W], 0.0).then_inc(s_ones, 1)
            dve.wait_ge(s_ones, 6)
            for n in range(2):
                V.memset(h_e[n][:, :, D:D + 1], 1.0).then_inc(s_ones, 1)
            dve.wait_ge(s_keys, 64)
            dve.wait_ge(s_mask, 3)
            V.memset(both_keys[:, ROUNDS:, :], 0)
            V.memset(x_rows[:, ROUNDS:, :], 0)
            for n, key in enumerate((src_key, dst_key)):
                one = slice(n * TILES, (n + 1) * TILES)
                half = keys_f[:, n * ROUNDS:(n + 1) * ROUNDS]
                V.tensor_copy(half[:, :, 0:TILES], key[:])
                V.tensor_tensor(half[:, :, TILES:], spare[:], key[:], ALU.subtract)
                V.tensor_scalar(x_rows[:, 0:ROUNDS, one], key[:], float(N - 1), None, ALU.min).then_inc(x_rows_ready, 1)
                link(V.tensor_copy(both_keys[:, 0:ROUNDS, one], key[:]))

            V.tensor_copy(keys_f[:, 2 * ROUNDS, :], keys_f[:, ROUNDS, :])
            dve.wait_ge(s_w, 16 * 9)
            link(V.tensor_copy(b2part[:, 0, :], b2f[:]))
            link(V.tensor_tensor(b2rest[:, 0, :], b2f[:], b2part[:, 0, :], ALU.subtract))
            link(V.tensor_copy(b2part[:, 1, :], b2rest[:, 0, :]))
            link(V.tensor_tensor(b2rest[:, 1, :], b2rest[:, 0, :], b2part[:, 1, :], ALU.subtract))
            link(V.tensor_copy(b2part[:, 2, :], b2rest[:, 1, :]))
            link(V.tensor_scalar(b2sel[:], b2part[:, 0, :], ident[0:3, 0:1], None, ALU.mult))
            for n in (1, 2):
                link(V.scalar_tensor_tensor(out=b2sel[:], in0=b2part[:, n, :], scalar=ident[0:3, n:n + 1], in1=b2sel[:],
                                            op0=ALU.mult, op1=ALU.add))
            V.tensor_copy(b2rows[:], b2sel[:].unsqueeze(1).broadcast_to([3, 8, D])).then_inc(s_b2, 1)

            def stage(rows, table, c, ready, width=2 * TILES):
                V.tensor_copy(rows[:], table[:, c, 0:width]).then_inc(ready, 1)

            def stage_first(rows, table, ready, width=2 * TILES):
                for n in range(LEAD):
                    stage(rows[n], table, n, ready, width)

            def stage_keys(k, slot):
                V.tensor_copy(key_col[k % 2][:], keys_f[:, slot, :]).then_inc(key_staged, 1)

            stage_keys(0, 0)

            def compare(b, k, sums_only=False):
                dve.wait_ge(key_staged, b + 1)
                dve.wait_ge(key_rows, b + 1)
                if k >= 2:
                    dve.wait_ge(sum_done, b - 1)
                for j in range(TILES):
                    w = (j + 1) * P
                    if sums_only:
                        ins = V.tensor_scalar(same[k % 2][:, j, 0:w], key_row[k % 2][:, 0:w], key_col[k % 2][:, j:j + 1],
                                              None, ALU.is_equal)
                    else:
                        ins = V.scalar_tensor_tensor(out=same[k % 2][:, j, 0:w], in0=key_row[k % 2][:, 0:w],
                                                     scalar=key_col[k % 2][:, j:j + 1], in1=upto[:, (TILES - 1 - j) * P:],
                                                     op0=ALU.is_equal, op1=ALU.mult, accum_out=count[:, j:j + 1])
                ins.then_inc(same_done, 1)

            def target(b, k, keep=None):
                dve.wait_ge(same_done, b + 1)
                if k >= NB:
                    dve.wait_ge(scattered, 64 * (b - NB + 1))
                key = key_col[k % 2]
                link(V.scalar_tensor_tensor(out=pushed[:], in0=count[:], scalar=1.0, in1=key[:, TILES:], op0=ALU.is_gt, op1=ALU.mult))
                if keep is not None:
                    V.tensor_tensor(keep, pushed[:], key[:, 0:TILES], ALU.add)
                V.tensor_tensor(sum_row[k % NB][:], pushed[:], key[:, 0:TILES], ALU.add).then_inc(row_ready, 1)

            def statistics(of, n, also=lambda: None, then=lambda: None):
                for r in range(n):
                    ins = V.bn_stats(stats[:, r, :], of[:, r, :])
                landed = chain.mark(ins)
                also()
                chain.wait(landed)
                even, odd = stats[:, 0:n, 0:3], stats[:, 0:n, 3:6]
                V.tensor_tensor(mean2[:, 0:n], even[:, :, 1], odd[:, :, 1], ALU.add)
                landed = chain.mark(V.tensor_tensor(diff[:, 0:n], even[:, :, 1], odd[:, :, 1], ALU.subtract))
                V.tensor_tensor(ssq2[:, 0:n], even[:, :, 2], odd[:, :, 2], ALU.add)
                then()
                chain.wait(landed)
                link(V.scalar_tensor_tensor(out=diff[:, 0:n], in0=diff[:, 0:n], scalar=float(D // 4), in1=diff[:, 0:n], op0=ALU.mult, op1=ALU.mult))
                V.tensor_tensor(ssq[:, 0:n], ssq2[:, 0:n], diff[:, 0:n], ALU.add).then_inc(ssq_ready, 1)

            def centre(of, to, n):
                return V.scalar_tensor_tensor(out=to, in0=bcast(mean2[:, 0:n], D), scalar=-0.5, in1=of, op0=ALU.mult, op1=ALU.add)

            def normalise(of, to, middle, n, r):
                link(centre(of, middle, n))
                dve.wait_ge(rstd_ready, r + 1)
                return V.scalar_tensor_tensor(out=to, in0=middle, scalar=0.0, in1=bcast(rstd[:, 0:n], D), op0=ALU.max, op1=ALU.mult)

            def by_head(t):
                return t.rearrange("p t (h d) -> p t h d", h=HEADS)

            def scores(i, k):
                dve.wait_ge(qkv_done, i + 1)
                dve.wait_ge(q_copied, i + 1)
                link(V.tensor_tensor(qk[:].rearrange("p (a t) d -> p a t d", a=2), QKV[:, :, :, D:2 * D],
                                     q_sb[:].rearrange("p (a t) d -> p a t d", a=2), ALU.mult))
                link(V.reduce_sum(att[:], by_head(qk[:]), axis=AX.X))
                V.tensor_scalar(att_c[:], att[:], 10.0, -10.0, ALU.min, ALU.max).then_inc(att_ready, 1)

            def weighted(i, k):
                dve.wait_ge(exp_ready, i + 1)
                for a in range(2):
                    tiles = slice(2 * a, 2 * a + 2)
                    ins = V.tensor_tensor(by_head(vals[k % 2][:, tiles, 0:D]), by_head(QKV[:, a, :, 2 * D:3 * D]),
                                          bcast(vals[k % 2][:, tiles, D:W], HD), ALU.mult)
                ins.then_inc(vals_ready, 1)

            def attention(i, k, g):
                if k + LEAD >= LATE:
                    stage(rows_x[(k + LEAD) % NB], x_rows, i + LEAD, rx_ready)
                pair, got, landed = pair_of(k, g)
                dve.wait_ge(got, landed)
                pair = pair.rearrange("p j e d -> p (j e) d")
                statistics(pair, 2 * TILES)
                stage_keys(k + 1, i + 1)
                compare(i, k)
                if k:
                    scores(i - 1, k - 1)
                normalise(pair, h_pair.rearrange("p j e d -> p (j e) d"), h_mid.rearrange("p j e d -> p (j e) d"),
                          2 * TILES, i).then_inc(h_ready, 1)
                if k:
                    weighted(i - 1, k - 1)
                target(i, k)

            rounds(dve, attention, chain, first=2, peel=EARLY.stop)
            scores(ROUNDS - 1, ROUNDS - 1)
            weighted(ROUNDS - 1, ROUNDS - 1)

            stage_first(rows_att, both_keys, ra_ready, TILES)
            dve.wait_ge(kept_x, ROUNDS)

            def sage(i, k, g):
                n, b, kb = k % NB, i + ROUNDS, k + ROUNDS
                stage(rows_att[(k + LEAD) % NB], both_keys, i + LEAD, ra_ready, TILES)
                got, sums_n = att_got[n], tb[n]
                dve.wait_ge(got_att[n], (g + k // NB + 1) * 64)
                e_sum = chain.mark(V.tensor_scalar(z_inv[:], got[:, :, D:W], 1e-8, None, ALU.add))
                dve.wait_ge(loaded[n], (g + k // NB + 1) * 32)
                n_sum = chain.mark(V.tensor_scalar(zn[:], sums_n[:, :, D:W], 1e-8, None, ALU.add))
                chain.wait(e_sum)
                e_inv = chain.mark(V.reciprocal(z_inv[:], z_inv[:]))
                chain.wait(n_sum)
                n_inv = chain.mark(V.reciprocal(zn[:], zn[:]))
                chain.wait(e_inv)
                e_mul = chain.mark(V.tensor_tensor(by_head(x1_e[:]), by_head(got[:, :, 0:D]), bcast(z_inv[:], HD), ALU.mult))
                chain.wait(n_inv)
                n_mul = chain.mark(V.tensor_tensor(by_head(sums_n[:, :, 0:D]), by_head(sums_n[:, :, 0:D]), bcast(zn[:], HD), ALU.mult))
                chain.wait(e_mul)
                e_add = chain.mark(V.tensor_tensor(x1_e[:], x1_e[:], edge[:, bass.ts(i, TILES), :], ALU.add))
                chain.wait(n_mul)
                V.tensor_tensor(xb[n][:], xb[n][:], sums_n[:, :, 0:D], ALU.add).then_inc(x1_ready, 1)
                chain.wait(e_add)
                dve.wait_ge(rstd_ready, b)
                statistics(x1_e[:], TILES)
                stage_keys(kb + 1, b + 1)
                if k >= 2:
                    dve.wait_ge(he_ready, i - 1)
                centre(x1_e[:], x_mid[k % 2], TILES).then_inc(xm_ready, 1)
                compare(b, kb)
                target(b, kb, dst_row[:, i, :])

            rounds(dve, sage, chain)

            stage_first(rows_agg, both_keys, rg_ready)
            dve.wait_ge(sum_done, 2 * ROUNDS)
            dve.wait_ge(s_z1, 16 * ROUNDS)
            dve.wait_ge(s_zo, 16)

            def output(i, k):
                n = k % NB
                for half in range(2):
                    rows8 = slice(8 * half, 8 * half + 8)
                    dve.wait_ge(w2_done, i * 4 + 2 * half + 2)
                    V.tensor_tensor(xb[n][:, rows8, :], xb[n][:, rows8, :], Y[k % 2][half].rearrange("p (r d) -> p r d", d=D),
                                    ALU.add).then_inc(y_read, 1)

            def nodes(i, k, g):
                u, n = k % 2, k % NB
                dve.wait_ge(loaded[n], (g + k // NB + 1) * 32 + 32 * len(range(n, ROUNDS, NB)))
                at_least_1 = None

                def counts():
                    nonlocal at_least_1
                    at_least_1 = chain.mark(V.tensor_scalar(inv_n[:], tb[n][:, :, D], 1.0, None, ALU.max))

                def inverse():
                    chain.wait(at_least_1)
                    chain.mark(V.reciprocal(inv_n[:], inv_n[:]))

                statistics(xb[n][:], ROWS, counts, inverse)
                if k >= 2:
                    dve.wait_ge(catT_done, i * 4 - 4)
                V.tensor_tensor(cat[u][:, :, 0, :], tb[n][:, :, 0:D], bcast(inv_n[:], D), ALU.mult)
                normalise(xb[n][:], cat[u][:, :, 1, :], mid, ROWS, i + 2 * ROUNDS).then_inc(cat_ready, 1)
                if k:
                    dve.wait_ge(agg_kept, i)
                stage(rows_agg[(k + LEAD) % NB], both_keys, i + LEAD, rg_ready)
                if k >= 2:
                    output(i - 2, k - 2)

            rounds(dve, nodes, chain)
            output(ROUNDS - 2, ROUNDS - 2)
            dve.wait_ge(agg_kept, ROUNDS)
            link(V.tensor_scalar(inv[:], inv[:], 1.0, None, ALU.max))
            link(V.reciprocal(inv[:], inv[:]))

            def means(i, k):
                if k >= 2:
                    dve.wait_ge(msgT_done, i - 1)
                V.tensor_tensor(cat_e[k % 2][:, :, 0, :], agg[:, bass.ts(i, TILES), :], bcast(inv[:, i, 0:TILES], D),
                                ALU.mult).then_inc(cat_e_agg, 1)

            def message(i, k):
                dve.wait_ge(w2l_done, i + 1)
                if k >= 2:
                    dve.wait_ge(sum_done, i - 1 + 2 * ROUNDS)
                V.tensor_tensor(msg[k % 2], MSG[k % 2][:, 0:TILES * D].rearrange("p (t d) -> p t d", d=D),
                                bcast(inv[:, i, TILES:], D), ALU.mult).then_inc(msg_ready, 1)

            def last_sums(i, k, g):
                b, kb = i + 2 * ROUNDS, k + 2 * ROUNDS
                means(i, k)
                if k == 0:
                    output(ROUNDS - 1, ROUNDS - 1)
                dve.wait_ge(same_done, b)
                stage_keys(kb + 1, i + ROUNDS + 1)
                dve.wait_ge(scattered, 64 * (b - NB + 1))
                V.tensor_copy(sum_row[kb % NB][:], dst_row[:, i, :]).then_inc(row_ready, 1)
                if k >= 2:
                    message(i - 2, k - 2)
                compare(b, kb, sums_only=True)

            rounds(dve, last_sums, chain)
            message(ROUNDS - 2, ROUNDS - 2)
            message(ROUNDS - 1, ROUNDS - 1)

        @block.scalar
        def _(act):
            chain = Chain(act, a_step)

            def copy_keys(b, k):
                act.wait_ge(keys_T, b + 1)
                if k >= 2:
                    act.wait_ge(same_done, b - 1)
                A.copy(key_row[k % 2][:], KEYS[:, :]).then_inc(key_rows, 1)

            def rsqrt(n, r):
                act.wait_ge(ssq_ready, r + 1)
                chain.link(A.activation(logv[:, 0:n], ssq[:, 0:n], ACT.Ln, bias=eps[:, 0:1], scale=1.0 / D))
                A.activation(rstd[:, 0:n], logv[:, 0:n], ACT.Exp, scale=-0.5).then_inc(rstd_ready, 1)

            def copy_sums(b, k, to, width):
                act.wait_ge(sum_done, b + 1)
                if k >= NB:
                    act.wait_ge(scattered, 64 * (b - NB + 1))
                A.copy(to[k % NB][:, :, :].rearrange("p t w -> p (t w)"), SUMS[k % 2][:, 0:TILES * width]).then_inc(sums_ready, 1)

            A.preload_act_table_set("natural_log_exp_and_others")
            act.wait_ge(s_ones, 8)
            act.wait_ge(s_w, 16 * 9)

            def q_and_exp(i, k):
                act.wait_ge(qkv_done, i + 1)
                if k:
                    act.wait_ge(att_ready, i)
                A.copy(q_sb[:].rearrange("p (a t) d -> p a t d", a=2), QKV[:, :, :, 0:D]).then_inc(q_copied, 1)
                act.wait_ge(att_ready, i + 1)
                if k >= 2:
                    act.wait_ge(sum_done, i - 1)
                A.activation(vals[k % 2][:, :, D:W], att_c[:], ACT.Exp).then_inc(exp_ready, 1)

            copy_keys(0, 0)

            def attention(i, k, g):
                pair, got, landed = pair_of(k, g)
                act.wait_ge(got, landed)
                A.copy(edge[:, bass.ts(i, TILES), :], pair[:, :, 0, :]).then_inc(kept_x, 1)
                rsqrt(2 * TILES, i)
                if k:
                    q_and_exp(i - 1, k - 1)
                act.wait_ge(hT_done, i + 1)
                A.copy(hT[:], HT[:, :]).then_inc(hT_copied, 1)
                if k:
                    copy_sums(i - 1, k - 1, sums, W)
                copy_keys(i + 1, k + 1)

            rounds(act, attention, chain, peel=EARLY.stop)
            q_and_exp(ROUNDS - 1, ROUNDS - 1)
            copy_sums(ROUNDS - 1, ROUNDS - 1, sums, W)

            def sage(i, k, g):
                b, kb = i + ROUNDS, k + ROUNDS
                rsqrt(TILES, b)
                act.wait_ge(rstd_ready, b + 1)
                act.wait_ge(xm_ready, i + 1)
                if k >= 2:
                    act.wait_ge(sum_done, b - 1)
                    act.wait_ge(kept_h, i - 1)
                for j in range(TILES):
                    ins = A.activation(h_e[k % 2][:, j, 0:D], x_mid[k % 2][:, j, :], ACT.Relu, scale=rstd[:, j:j + 1])
                ins.then_inc(he_ready, 1)
                act.wait_ge(he_ready, i + 1)
                A.copy(edge[:, bass.ts(i, TILES), :], h_e[k % 2][:, :, 0:D]).then_inc(kept_h, 1)
                copy_keys(b + 1, kb + 1)
                copy_sums(b, kb, sums, W)

            rounds(act, sage, chain)
            act.wait_ge(kept_h, ROUNDS)

            def group(i, k, q):
                n, kn = i * 4 + q, k * 4 + q
                act.wait_ge(catT_done, n + 1)
                if kn >= 2:
                    act.wait_ge(g_done, n - 1)
                A.copy(catT[kn % 2][:], CATT[:, kn % 2, :]).then_inc(catT_copied, 1)
                if kn:
                    relu(n - 1, kn - 1)

            def relu(n, kn):
                act.wait_ge(g_done, n + 1)
                if kn >= 2:
                    act.wait_ge(w2_done, n - 1)
                A.activation(gT[kn % 2][:], G[kn % 2], ACT.Relu, bias=b1c[:, 0:1]).then_inc(g_ready, 1)

            def nodes(i, k, g):
                if k:
                    group(i - 1, k - 1, 0)
                    group(i - 1, k - 1, 1)
                rsqrt(ROWS, i + 2 * ROUNDS)
                act.wait_ge(got_agg[k % NB], (g + k // NB + 1) * 128)
                A.copy(agg[:, bass.ts(i, TILES), :], agg_got[k % NB][:, 0:TILES, 0:D])
                A.copy(inv[:, i, :], agg_got[k % NB][:, :, D]).then_inc(agg_kept, 1)
                if k:
                    group(i - 1, k - 1, 2)
                    group(i - 1, k - 1, 3)

            rounds(act, nodes, chain)
            for q in range(4):
                group(ROUNDS - 1, ROUNDS - 1, q)
            relu(4 * ROUNDS - 1, 4 * ROUNDS - 1)

            def edge_h(i, k):
                if k >= 2:
                    act.wait_ge(msgT_done, i - 1)
                A.copy(cat_e[k % 2][:, :, 1, :], edge[:, bass.ts(i, TILES), :]).then_inc(cat_e_h, 1)

            def edge_group(i, k):
                act.wait_ge(msgT_done, i + 1)
                if k:
                    act.wait_ge(eg_done, i)
                A.copy(catT[0][:], CATT[:, 0, :]).then_inc(msgT_copied, 1)

            def edge_relu(i, k):
                act.wait_ge(eg_done, i + 1)
                if k >= 2:
                    act.wait_ge(w2l_done, i - 1)
                A.activation(gT[k % 2][:], G[0], ACT.Relu, bias=b1c[:, 0:1]).then_inc(eg_ready, 1)

            act.wait_ge(w2_done, 4 * ROUNDS - 1)

            def last_sums(i, k, g):
                b, kb = i + 2 * ROUNDS, k + 2 * ROUNDS
                edge_h(i, k)
                edge_group(i, k)
                if k >= 2:
                    copy_sums(b - 2, kb - 2, sums_out, D)
                edge_relu(i, k)
                copy_keys(b + 1, kb + 1)

            rounds(act, last_sums, chain)
            for b in (3 * ROUNDS - 2, 3 * ROUNDS - 1):
                copy_sums(b, b, sums_out, D)

        @block.tensor
        def _(pe):
            def transpose_keys(b, k):
                pe.wait_ge(key_staged, b + 1)
                if k:
                    pe.wait_ge(key_rows, b)
                for j in range(TILES):
                    ins = T.transpose(KEYS[:, j * P:(j + 1) * P], key_col[k % 2][:, j:j + 1].broadcast_to([P, P]), ident[:])
                ins.then_inc(keys_T, 1)

            def sum_up(b, k, values, width):
                pe.wait_ge(same_done, b + 1)
                if k >= 2:
                    pe.wait_ge(sums_ready, b - 1)
                for i in range(TILES):
                    for j in range(i, TILES):
                        ins = T.matmul(SUMS[k % 2][:, i * width:(i + 1) * width], same[k % 2][:, j, i * P:(i + 1) * P],
                                       values(j), start=(j == i), stop=(j == TILES - 1))
                ins.then_inc(sum_done, 1)

            pe.wait_ge(s_mask, 3)
            pe.wait_ge(s_ones, 8)
            pe.wait_ge(s_w, 16 * 9)

            transpose_keys(0, 0)

            def sum_attention(i, k):
                pe.wait_ge(vals_ready, i + 1)
                sum_up(i, k, lambda j: vals[k % 2][:, j, :], W)

            def attention(i, k, g):
                pe.wait_ge(h_ready, i + 1)
                if k:
                    pe.wait_ge(hT_copied, i)
                for j in range(TILES):
                    ins = T.transpose(HT[:, j * P:(j + 1) * P], h_pair[:, j].rearrange("p e d -> p (e d)"), ident[:])
                ins.then_inc(hT_done, 1)
                if k:
                    sum_attention(i - 1, k - 1)
                transpose_keys(i + 1, k + 1)
                pe.wait_ge(hT_copied, i + 1)
                for j in range(TILES):
                    ins = T.matmul(QKV[:, j // 2, j % 2, :], hT[:, j * P:(j + 1) * P], wqkv[:], start=True, stop=True)
                ins.then_inc(qkv_done, 1)

            rounds(pe, attention, peel=EARLY.stop)
            sum_attention(ROUNDS - 1, ROUNDS - 1)

            def sage(i, k, g):
                b, kb = i + ROUNDS, k + ROUNDS
                transpose_keys(b + 1, kb + 1)
                pe.wait_ge(he_ready, i + 1)
                sum_up(b, kb, lambda j: h_e[k % 2][:, j, :], W)

            rounds(pe, sage)

            pe.wait_ge(sums_ready, 2 * ROUNDS)
            pe.wait_ge(key_rows, 2 * ROUNDS + 1)
            pe.wait_ge(s_b2, 1)

            def times_w1(n, kn):
                pe.wait_ge(catT_copied, n + 1)
                if kn >= 2:
                    pe.wait_ge(g_ready, n - 1)
                T.matmul(G[kn % 2], w1[:], catT[kn % 2][:], start=True, stop=True).then_inc(g_done, 1)

            def times_w2(i, k, q):
                n, kn = i * 4 + q, k * 4 + q
                pe.wait_ge(g_ready, n + 1)
                half = q // 2
                to = Y[k % 2][half]
                if q % 2 == 0:
                    if k >= 2:
                        pe.wait_ge(y_read, i * 2 + half - 3)
                    T.matmul(to, ones3[:], b2rows[:].rearrange("p a d -> p (a d)"), start=True, stop=False)
                for t in range(4):
                    at = (q % 2 * 4 + t) * D
                    ins = T.matmul(to[:, at:at + D], gT[kn % 2][:, t * P:(t + 1) * P], w2r[:], start=False,
                                   stop=(q % 2 == 1 and t == 3))
                ins.then_inc(w2_done, 1)

            def nodes(i, k, g):
                for q in range(4):
                    n, kn = i * 4 + q, k * 4 + q
                    if q == 0:
                        pe.wait_ge(cat_ready, i + 1)
                    if kn >= 2:
                        pe.wait_ge(catT_copied, n - 1)
                    for t in range(4):
                        ins = T.transpose(CATT[:, kn % 2, t * P:(t + 1) * P], cat[k % 2][:, 4 * q + t].rearrange("p e d -> p (e d)"), ident[:])
                    ins.then_inc(catT_done, 1)
                    if kn >= 1:
                        times_w1(n - 1, kn - 1)
                    if kn >= 2:
                        if q >= 2:
                            times_w2(i, k, q - 2)
                        else:
                            times_w2(i - 1, k - 1, q + 2)

            rounds(pe, nodes)
            times_w1(4 * ROUNDS - 1, 4 * ROUNDS - 1)
            times_w2(ROUNDS - 1, ROUNDS - 1, 2)
            times_w2(ROUNDS - 1, ROUNDS - 1, 3)

            pe.wait_ge(catT_copied, 4 * ROUNDS)
            pe.wait_ge(g_ready, 4 * ROUNDS)

            def edge_transposes(i, k):
                pe.wait_ge(cat_e_agg, i + 1)
                pe.wait_ge(cat_e_h, i + 1)
                if k:
                    pe.wait_ge(msgT_copied, i)
                for t in range(TILES):
                    ins = T.transpose(CATT[:, 0, t * P:(t + 1) * P], cat_e[k % 2][:, t].rearrange("p e d -> p (e d)"), ident[:])
                ins.then_inc(msgT_done, 1)

            def edge_w1(i, k):
                pe.wait_ge(msgT_copied, i + 1)
                if k:
                    pe.wait_ge(eg_ready, i)
                T.matmul(G[0], w1[:], catT[0][:], start=True, stop=True).then_inc(eg_done, 1)

            def edge_w2(i, k):
                pe.wait_ge(eg_ready, i + 1)
                if k >= 2:
                    pe.wait_ge(msg_ready, i - 1)
                for t in range(TILES):
                    ins = T.matmul(MSG[k % 2][:, t * D:(t + 1) * D], gT[k % 2][:, t * P:(t + 1) * P], w2l[:], start=True, stop=True)
                ins.then_inc(w2l_done, 1)

            def sum_messages(i, k):
                b, kb = i + 2 * ROUNDS, k + 2 * ROUNDS
                pe.wait_ge(msg_ready, i + 1)
                sum_up(b, kb, lambda j: msg[k % 2][:, j, :], D)

            def last_sums(i, k, g):
                edge_transposes(i, k)
                if k >= 2:
                    sum_messages(i - 2, k - 2)
                edge_w1(i, k)
                if k == 0:
                    pe.wait_ge(y_read, 2 * ROUNDS)
                transpose_keys(i + 2 * ROUNDS + 1, k + 2 * ROUNDS + 1)
                if k:
                    edge_w2(i - 1, k - 1)

            rounds(pe, last_sums)
            edge_w2(ROUNDS - 1, ROUNDS - 1)
            sum_messages(ROUNDS - 2, ROUNDS - 2)
            sum_messages(ROUNDS - 1, ROUNDS - 1)


_INS = ["x", "src", "dst", "L0_gnn_Wq", "L0_gnn_Wk", "L0_gnn_Wv", "L1_gnn_W1l", "L1_gnn_b1", "L1_gnn_W1r",
        "L1_gnn_W2l", "L1_gnn_b2", "L1_gnn_W2r"]


def kernel(**inputs):
    import numpy as np
    import concourse.bacc as bacc
    from concourse.bass_utils import run_bass_kernel_spmd

    nc = bacc.Bacc("TRN2", target_bir_lowering=False, num_devices=1)
    arrays, args = {}, []
    for name in _INS:
        a = np.ascontiguousarray(inputs[name])
        arrays[f"in_{name}"] = a
        args.append(nc.dram_tensor(f"in_{name}", a.shape, mybir.dt.from_np(a.dtype), kind="ExternalInput").ap())
    out = nc.dram_tensor("out", (TABLE, D), mybir.dt.float32, kind="ExternalOutput").ap()
    gnn_kernel(nc, *args, out)
    r = run_bass_kernel_spmd(nc, [arrays], core_ids=[0])
    return r.results[0]["out"][0:N]
```
